# Optimizing a Trainium2 kernel written in Bass

```python
import numpy as np
import jax
import jax.numpy as jnp

def _softmax(x, axis=-1):
    return jax.nn.softmax(x, axis=axis)

def _gelu(x):
    return jax.nn.gelu(x, approximate=True)

def _silu(x):
    return jax.nn.silu(x)

def _sigmoid(x):
    return jax.nn.sigmoid(x)

def _layernorm(x, axis=-1, eps=1e-05):
    m = jnp.mean(x, axis=axis, keepdims=True)
    v = jnp.var(x, axis=axis, keepdims=True)
    return (x - m) / jnp.sqrt(v + eps)

def _scatter_add(tgt, idx, src, axis=0):
    return tgt.at[idx].add(src)

def _segment_sum(src, seg, n):
    return jax.ops.segment_sum(src, seg, n)
kernel_name = 'mk_adj_seq_d4_adj_r2_72b908'

def setup_inputs(seed: int=0):
    np.random.seed(seed)
    _w = jnp.asarray

    def _rec_inputs():
        import jax
        import jax.numpy as jnp
        _gk = jax.random.key(seed)
        x = -0.0005207 + 1.001 * jax.random.normal(jax.random.fold_in(_gk, 1), (32, 256, 256), jnp.float32)
        _a = jax.random.bernoulli(jax.random.fold_in(_gk, 2), 0.0078125, (32, 256, 256))
        _a = jnp.logical_or(_a, jnp.swapaxes(_a, -1, -2))
        _a = jnp.logical_or(_a, jnp.eye(256, dtype=bool))
        adj = _a.astype(jnp.int32)
        return (x, adj)
    x, adj = _rec_inputs()

    def _L0_gnn_setup():
        import jax, jax.numpy as jnp
        import numpy as np
        B, S, D, H = (2, 1024, 256, 8)
        HD = D // H
        EPS = 1e-05

        def _ln(x, g, b):
            mu = jnp.mean(x, axis=-1, keepdims=True)
            var = jnp.mean((x - mu) ** 2, axis=-1, keepdims=True)
            return (x - mu) * jax.lax.rsqrt(var + EPS) * g + b
        key = jax.random.key(seed)
        ks = jax.random.split(key, 16)
        x = jax.random.normal(ks[0], (B, S, D), dtype=jnp.float32)
        adj = jax.random.randint(ks[1], (B, S, S), 0, 2, dtype=jnp.int32)
        adj = adj.at[:, jnp.arange(S), jnp.arange(S)].set(1)
        edge_attr = jax.random.normal(ks[2], (B, S, S), dtype=jnp.float32)
        sc = 1.0 / np.sqrt(D)
        p = lambda k, shp: jax.random.normal(k, shp, dtype=jnp.float32) * sc
        return {'x': x, 'adj_matrix': adj, 'edge_attr_matrix': edge_attr, 'ln1_g': jnp.ones((D,)), 'ln1_b': jnp.zeros((D,)), 'ln2_g': jnp.ones((D,)), 'ln2_b': jnp.zeros((D,)), 'wq': p(ks[3], (D, D)), 'bq': jnp.zeros((D,)), 'wk': p(ks[4], (D, D)), 'bk': jnp.zeros((D,)), 'wv': p(ks[5], (D, D)), 'bv': jnp.zeros((D,)), 'wo': p(ks[6], (D, D)), 'bo': jnp.zeros((D,)), 'w1': p(ks[7], (D, 4 * D)), 'b1': jnp.zeros((4 * D,)), 'w2': p(ks[8], (4 * D, D)), 'b2': jnp.zeros((D,))}
    _L0_gnn_all = _L0_gnn_setup()
    _L0_gnn_in = {k: v for k, v in _L0_gnn_all.items() if k in ('ln1_g', 'ln1_b', 'ln2_g', 'ln2_b', 'wq', 'bq', 'wk', 'bk', 'wv', 'bv', 'wo', 'bo', 'w1', 'b1', 'w2', 'b2')}
    del _L0_gnn_all

    def _L1_gnn_setup():
        import jax, jax.numpy as jnp
        import numpy as np
        B, N, D, H = (4, 1024, 256, 8)
        HD = D // H
        EPS = 1e-05
        key = jax.random.key(seed)
        ks = jax.random.split(key, 12)
        x = jax.random.normal(ks[0], (B, N, D), dtype=jnp.float32)
        adj = jax.random.randint(ks[1], (B, N, N), 0, 2, dtype=jnp.int32)
        adj = jnp.maximum(adj, jnp.eye(N, dtype=jnp.int32)[None, :, :])
        s = 1.0 / np.sqrt(D)
        Wq = jax.random.uniform(ks[2], (D, D), jnp.float32, -s, s)
        bq = jnp.zeros((D,), jnp.float32)
        Wk = jax.random.uniform(ks[3], (D, D), jnp.float32, -s, s)
        bk = jnp.zeros((D,), jnp.float32)
        Wv = jax.random.uniform(ks[4], (D, D), jnp.float32, -s, s)
        bv = jnp.zeros((D,), jnp.float32)
        Wo = jax.random.uniform(ks[5], (D, D), jnp.float32, -s, s)
        bo = jnp.zeros((D,), jnp.float32)
        gamma = jnp.ones((D,), jnp.float32)
        beta = jnp.zeros((D,), jnp.float32)
        return {'x': x, 'adj': adj, 'Wq': Wq, 'bq': bq, 'Wk': Wk, 'bk': bk, 'Wv': Wv, 'bv': bv, 'Wo': Wo, 'bo': bo, 'gamma': gamma, 'beta': beta}
    _L1_gnn_all = _L1_gnn_setup()
    _L1_gnn_in = {k: v for k, v in _L1_gnn_all.items() if k in ('Wq', 'bq', 'Wk', 'bk', 'Wv', 'bv', 'Wo', 'bo', 'gamma', 'beta')}
    del _L1_gnn_all

    def _L2_gnn_setup():
        import jax, jax.numpy as jnp
        import numpy as np
        import math
        D = 256
        B, L = (8, 1024)
        EPS = 1e-05

        def layer_norm(y, gamma, beta):
            mu = jnp.mean(y, axis=-1, keepdims=True)
            var = jnp.mean(jnp.square(y - mu), axis=-1, keepdims=True)
            return (y - mu) * jax.lax.rsqrt(var + EPS) * gamma + beta
        key = jax.random.key(seed)
        ks = jax.random.split(key, 8)
        s = 1.0 / math.sqrt(D)
        x = jax.random.normal(ks[0], (B, L, D), dtype=jnp.float32)
        adj = jax.random.randint(ks[1], (B, L, L), 0, 2, dtype=jnp.int32)
        Wq = jax.random.normal(ks[2], (D, D), dtype=jnp.float32) * s
        Wk = jax.random.normal(ks[3], (D, D), dtype=jnp.float32) * s
        Wv = jax.random.normal(ks[4], (D, D), dtype=jnp.float32) * s
        Wo = jax.random.normal(ks[5], (D, D), dtype=jnp.float32) * s
        bo = jnp.zeros((D,), dtype=jnp.float32)
        gamma = jnp.ones((D,), dtype=jnp.float32)
        beta = jnp.zeros((D,), dtype=jnp.float32)
        return {'x': x, 'adj': adj, 'Wq': Wq, 'Wk': Wk, 'Wv': Wv, 'Wo': Wo, 'bo': bo, 'gamma': gamma, 'beta': beta}
    _L2_gnn_all = _L2_gnn_setup()
    _L2_gnn_in = {k: v for k, v in _L2_gnn_all.items() if k in ('Wq', 'Wk', 'Wv', 'Wo', 'bo', 'gamma', 'beta')}
    del _L2_gnn_all

    def _L3_gnn_setup():
        import jax, jax.numpy as jnp
        import numpy as np
        B, N, H, D = (8, 512, 256, 4)
        EPS = 1e-08
        LN_EPS = 1e-05

        def _linear(x, W, b):
            return x @ W.T + b
        key = jax.random.key(seed)
        ks = jax.random.split(key, 20)
        inp = {'adj': jax.random.randint(ks[0], (B, N, N), 0, D + 1, dtype=jnp.int32), 'relative_pos': jax.random.randint(ks[1], (B, N, N), 0, 16, dtype=jnp.int32), 'hid': jax.random.normal(ks[2], (B, N, H), dtype=jnp.float32), 'Wd': jax.random.normal(ks[3], (H, D * H), dtype=jnp.float32) * (1.0 / np.sqrt(D * H)), 'bd': jnp.zeros((H,), jnp.float32)}
        s = 1.0 / np.sqrt(H)
        for i, nm in enumerate(['ri', 'rh', 'zi', 'zh', 'ni', 'nh']):
            inp['W' + nm] = jax.random.normal(ks[4 + i], (H, H), dtype=jnp.float32) * s
            inp['b' + nm] = jnp.zeros((H,), jnp.float32)
        inp['gamma'] = jnp.ones((H,), jnp.float32)
        inp['beta'] = jnp.zeros((H,), jnp.float32)
        return inp
    _L3_gnn_all = _L3_gnn_setup()
    _L3_gnn_in = {k: v for k, v in _L3_gnn_all.items() if k in ('Wd', 'bd', 'Wri', 'bri', 'Wrh', 'brh', 'Wzi', 'bzi', 'Wzh', 'bzh', 'Wni', 'bni', 'Wnh', 'bnh', 'gamma', 'beta')}
    del _L3_gnn_all
    return {'x': x, 'adj': adj, 'L0_gnn_ln1_g': _L0_gnn_in['ln1_g'], 'L0_gnn_ln1_b': _L0_gnn_in['ln1_b'], 'L0_gnn_ln2_g': _L0_gnn_in['ln2_g'], 'L0_gnn_ln2_b': _L0_gnn_in['ln2_b'], 'L0_gnn_wq': _L0_gnn_in['wq'], 'L0_gnn_bq': _L0_gnn_in['bq'], 'L0_gnn_wk': _L0_gnn_in['wk'], 'L0_gnn_bk': _L0_gnn_in['bk'], 'L0_gnn_wv': _L0_gnn_in['wv'], 'L0_gnn_bv': _L0_gnn_in['bv'], 'L0_gnn_wo': _L0_gnn_in['wo'], 'L0_gnn_bo': _L0_gnn_in['bo'], 'L0_gnn_w1': _L0_gnn_in['w1'], 'L0_gnn_b1': _L0_gnn_in['b1'], 'L0_gnn_w2': _L0_gnn_in['w2'], 'L0_gnn_b2': _L0_gnn_in['b2'], 'L1_gnn_Wq': _L1_gnn_in['Wq'], 'L1_gnn_bq': _L1_gnn_in['bq'], 'L1_gnn_Wk': _L1_gnn_in['Wk'], 'L1_gnn_bk': _L1_gnn_in['bk'], 'L1_gnn_Wv': _L1_gnn_in['Wv'], 'L1_gnn_bv': _L1_gnn_in['bv'], 'L1_gnn_Wo': _L1_gnn_in['Wo'], 'L1_gnn_bo': _L1_gnn_in['bo'], 'L1_gnn_gamma': _L1_gnn_in['gamma'], 'L1_gnn_beta': _L1_gnn_in['beta'], 'L2_gnn_Wq': _L2_gnn_in['Wq'], 'L2_gnn_Wk': _L2_gnn_in['Wk'], 'L2_gnn_Wv': _L2_gnn_in['Wv'], 'L2_gnn_Wo': _L2_gnn_in['Wo'], 'L2_gnn_bo': _L2_gnn_in['bo'], 'L2_gnn_gamma': _L2_gnn_in['gamma'], 'L2_gnn_beta': _L2_gnn_in['beta'], 'L3_gnn_Wd': _L3_gnn_in['Wd'], 'L3_gnn_bd': _L3_gnn_in['bd'], 'L3_gnn_Wri': _L3_gnn_in['Wri'], 'L3_gnn_bri': _L3_gnn_in['bri'], 'L3_gnn_Wrh': _L3_gnn_in['Wrh'], 'L3_gnn_brh': _L3_gnn_in['brh'], 'L3_gnn_Wzi': _L3_gnn_in['Wzi'], 'L3_gnn_bzi': _L3_gnn_in['bzi'], 'L3_gnn_Wzh': _L3_gnn_in['Wzh'], 'L3_gnn_bzh': _L3_gnn_in['bzh'], 'L3_gnn_Wni': _L3_gnn_in['Wni'], 'L3_gnn_bni': _L3_gnn_in['bni'], 'L3_gnn_Wnh': _L3_gnn_in['Wnh'], 'L3_gnn_bnh': _L3_gnn_in['bnh'], 'L3_gnn_gamma': _L3_gnn_in['gamma'], 'L3_gnn_beta': _L3_gnn_in['beta']}

def reference(x, adj, L0_gnn_ln1_g, L0_gnn_ln1_b, L0_gnn_ln2_g, L0_gnn_ln2_b, L0_gnn_wq, L0_gnn_bq, L0_gnn_wk, L0_gnn_bk, L0_gnn_wv, L0_gnn_bv, L0_gnn_wo, L0_gnn_bo, L0_gnn_w1, L0_gnn_b1, L0_gnn_w2, L0_gnn_b2, L1_gnn_Wq, L1_gnn_bq, L1_gnn_Wk, L1_gnn_bk, L1_gnn_Wv, L1_gnn_bv, L1_gnn_Wo, L1_gnn_bo, L1_gnn_gamma, L1_gnn_beta, L2_gnn_Wq, L2_gnn_Wk, L2_gnn_Wv, L2_gnn_Wo, L2_gnn_bo, L2_gnn_gamma, L2_gnn_beta, L3_gnn_Wd, L3_gnn_bd, L3_gnn_Wri, L3_gnn_bri, L3_gnn_Wrh, L3_gnn_brh, L3_gnn_Wzi, L3_gnn_bzi, L3_gnn_Wzh, L3_gnn_bzh, L3_gnn_Wni, L3_gnn_bni, L3_gnn_Wnh, L3_gnn_bnh, L3_gnn_gamma, L3_gnn_beta):
    import jax
    import jax.numpy as jnp

    def _L0_gnn_ref(x, adj_matrix, edge_attr_matrix, ln1_g, ln1_b, ln2_g, ln2_b, wq, bq, wk, bk, wv, bv, wo, bo, w1, b1, w2, b2):
        import jax, jax.numpy as jnp
        import numpy as np
        B, S, D, H = (2, 1024, 256, 8)
        HD = D // H
        EPS = 1e-05

        def _ln(x, g, b):
            mu = jnp.mean(x, axis=-1, keepdims=True)
            var = jnp.mean((x - mu) ** 2, axis=-1, keepdims=True)
            return (x - mu) * jax.lax.rsqrt(var + EPS) * g + b
        b, s, d = x.shape
        residual = x
        nx = _ln(x, ln1_g, ln1_b)
        q = (nx @ wq + bq).reshape(b, s, H, HD).transpose(0, 2, 1, 3)
        k = (nx @ wk + bk).reshape(b, s, H, HD).transpose(0, 2, 1, 3)
        v = (nx @ wv + bv).reshape(b, s, H, HD).transpose(0, 2, 1, 3)
        adjf = adj_matrix.astype(jnp.float32)
        bias = jnp.where(adj_matrix > 0, 0.1 * edge_attr_matrix * adjf, -jnp.inf)[:, None]
        scores = jnp.einsum('bhqd,bhkd->bhqk', q, k) / np.sqrt(HD) + bias
        attn = jax.nn.softmax(scores, axis=-1)
        out = jnp.einsum('bhqk,bhkd->bhqd', attn, v)
        out = out.transpose(0, 2, 1, 3).reshape(b, s, d)
        x1 = residual + (out @ wo + bo)
        n2 = _ln(x1, ln2_g, ln2_b)
        mlp = jax.nn.gelu(n2 @ w1 + b1, approximate=False) @ w2 + b2
        return x1 + mlp

    def _L1_gnn_ref(x, adj, Wq, bq, Wk, bk, Wv, bv, Wo, bo, gamma, beta):
        import jax, jax.numpy as jnp
        import numpy as np
        B, N, D, H = (4, 1024, 256, 8)
        HD = D // H
        EPS = 1e-05
        b, n, d = x.shape
        scale = 1.0 / np.sqrt(HD).astype(np.float32)
        q = (x @ Wq + bq).reshape(b, n, H, HD)
        k = (x @ Wk + bk).reshape(b, n, H, HD)
        v = (x @ Wv + bv).reshape(b, n, H, HD)
        scores = jnp.einsum('bnhd,bmhd->bhnm', q, k) * scale
        mask = (adj == 0)[:, None, :, :]
        scores = jnp.where(mask, jnp.float32(-jnp.inf), scores)
        attn = jax.nn.softmax(scores, axis=-1)
        h = jnp.einsum('bhnm,bmhd->bnhd', attn, v).reshape(b, n, d)
        h = h @ Wo + bo
        y = h + x
        mu = jnp.mean(y, axis=-1, keepdims=True)
        var = jnp.mean(jnp.square(y - mu), axis=-1, keepdims=True)
        return (y - mu) * jax.lax.rsqrt(var + EPS) * gamma + beta

    def _L2_gnn_ref(x, adj, Wq, Wk, Wv, Wo, bo, gamma, beta):
        import jax, jax.numpy as jnp
        import numpy as np
        import math
        D = 256
        B, L = (8, 1024)
        EPS = 1e-05

        def layer_norm(y, gamma, beta):
            mu = jnp.mean(y, axis=-1, keepdims=True)
            var = jnp.mean(jnp.square(y - mu), axis=-1, keepdims=True)
            return (y - mu) * jax.lax.rsqrt(var + EPS) * gamma + beta
        d_out = Wq.shape[1]
        scale = 1.0 / math.sqrt(d_out)
        Q = x @ Wq
        K = x @ Wk
        V = x @ Wv
        sc = jnp.einsum('bld,bmd->blm', Q, K) * scale
        mask = adj == 0
        sc = jnp.where(mask, -jnp.inf, sc)
        all_inf = jnp.all(mask, axis=-1, keepdims=True)
        sc = jnp.where(all_inf, 0.0, sc)
        w = jax.nn.softmax(sc, axis=-1)
        out = jnp.einsum('blm,bmd->bld', w, V)
        y = x + out @ Wo + bo
        return layer_norm(y, gamma, beta)

    def _L3_gnn_ref(adj, relative_pos, hid, Wd, bd, Wri, bri, Wrh, brh, Wzi, bzi, Wzh, bzh, Wni, bni, Wnh, bnh, gamma, beta):
        import jax, jax.numpy as jnp
        import numpy as np
        B, N, H, D = (8, 512, 256, 4)
        EPS = 1e-08
        LN_EPS = 1e-05

        def _linear(x, W, b):
            return x @ W.T + b
        dt = hid.dtype
        labels = jnp.arange(1, D + 1, dtype=adj.dtype)
        mask = (adj[None] == labels[:, None, None, None]).astype(dt)
        weight = mask / (jnp.sum(mask, axis=-1, keepdims=True) + EPS)
        agg = jnp.einsum('dbmn,bnh->bmdh', weight, hid).reshape(hid.shape[0], hid.shape[1], D * H)
        out = jax.nn.relu(_linear(agg, Wd, bd))
        r = jax.nn.sigmoid(_linear(out, Wri, bri) + _linear(hid, Wrh, brh))
        z = jax.nn.sigmoid(_linear(out, Wzi, bzi) + _linear(hid, Wzh, bzh))
        n = jnp.tanh(_linear(out, Wni, bni) + r * _linear(hid, Wnh, bnh))
        out = (1.0 - z) * n + z * hid
        mu = jnp.mean(out, axis=-1, keepdims=True)
        var = jnp.var(out, axis=-1, keepdims=True)
        return (out - mu) / jnp.sqrt(var + LN_EPS) * gamma + beta
    x = _L0_gnn_ref(x, adj, adj, L0_gnn_ln1_g, L0_gnn_ln1_b, L0_gnn_ln2_g, L0_gnn_ln2_b, L0_gnn_wq, L0_gnn_bq, L0_gnn_wk, L0_gnn_bk, L0_gnn_wv, L0_gnn_bv, L0_gnn_wo, L0_gnn_bo, L0_gnn_w1, L0_gnn_b1, L0_gnn_w2, L0_gnn_b2)
    x = _L1_gnn_ref(x, adj, L1_gnn_Wq, L1_gnn_bq, L1_gnn_Wk, L1_gnn_bk, L1_gnn_Wv, L1_gnn_bv, L1_gnn_Wo, L1_gnn_bo, L1_gnn_gamma, L1_gnn_beta)
    x = _L2_gnn_ref(x, adj, L2_gnn_Wq, L2_gnn_Wk, L2_gnn_Wv, L2_gnn_Wo, L2_gnn_bo, L2_gnn_gamma, L2_gnn_beta)
    x = _L3_gnn_ref(adj, adj, x, L3_gnn_Wd, L3_gnn_bd, L3_gnn_Wri, L3_gnn_bri, L3_gnn_Wrh, L3_gnn_brh, L3_gnn_Wzi, L3_gnn_bzi, L3_gnn_Wzh, L3_gnn_bzh, L3_gnn_Wni, L3_gnn_bni, L3_gnn_Wnh, L3_gnn_bnh, L3_gnn_gamma, L3_gnn_beta)
    return x

_drawn_inputs = setup_inputs


def setup_inputs(seed=0):
    import zlib

    import numpy as np

    out = dict(_drawn_inputs(seed))
    spreads = {'L0_gnn_ln1_g': (1.0, 0.2),
     'L0_gnn_ln1_b': (0.0, 0.1),
     'L0_gnn_ln2_g': (1.0, 0.2),
     'L0_gnn_ln2_b': (0.0, 0.1),
     'L0_gnn_bq': (0.0, 0.1),
     'L0_gnn_bk': (0.0, 0.8),
     'L0_gnn_bv': (0.0, 0.1),
     'L0_gnn_bo': (0.0, 0.1),
     'L0_gnn_b1': (0.0, 0.1),
     'L0_gnn_b2': (0.0, 0.1),
     'L1_gnn_bq': (0.0, 0.738),
     'L1_gnn_bk': (0.0, 0.8),
     'L1_gnn_bv': (0.0, 0.1),
     'L1_gnn_bo': (0.0, 0.1),
     'L1_gnn_gamma': (1.0, 0.2),
     'L1_gnn_beta': (0.0, 0.1),
     'L2_gnn_bo': (0.0, 0.1),
     'L2_gnn_gamma': (1.0, 0.2),
     'L2_gnn_beta': (0.0, 0.1),
     'L3_gnn_bd': (0.0, 0.1),
     'L3_gnn_bri': (0.0, 0.689),
     'L3_gnn_brh': (0.0, 0.691),
     'L3_gnn_bzi': (0.0, 0.1),
     'L3_gnn_bzh': (0.0, 0.1),
     'L3_gnn_bni': (0.0, 0.1),
     'L3_gnn_bnh': (0.0, 0.1),
     'L3_gnn_gamma': (1.0, 0.2),
     'L3_gnn_beta': (0.0, 0.1)}
    factors = {}
    for name, (base, spread) in spreads.items():
        noise = np.random.default_rng([zlib.crc32(name.encode()), seed]).standard_normal(out[name].shape)
        drawn = base * np.exp(spread * noise) if base else spread * noise
        out[name] = jnp.asarray(drawn.astype(out[name].dtype))
    for name, factor in factors.items():
        out[name] = (out[name] * factor).astype(out[name].dtype)
    return out
```

```python
from contextlib import ExitStack

import numpy as np

import concourse.bass as bass
from concourse import mybir

F32 = mybir.dt.float32
F32R = mybir.dt.float32r
I32 = mybir.dt.int32
ALU = mybir.AluOpType
ACT = mybir.ActivationFunctionType

P = 128
D = 256
DC = D // P
RT = D // P
W = RT * D
H = 8
HD = D // H
HPC = P // HD
FF = 4 * D
UPS = FF // P // 2
LABELS = 4
BIG = 1e38
QSCALE = float(1.0 / np.sqrt(HD))
LN_EPS = 1e-5
AGG_EPS = 1e-8

GROUPS = [["q0", "k0", "v0", "o0"], ["w1"], ["w2"], ["q1", "k1", "v1", "o1"],
          ["wd"], ["ri", "rh", "zi", "zh"], ["ni", "nh"], ["q2T", "k2T", "v2T", "o2"]]
WIDE = {"w1": 8, "w2": 8, "wd": 8}
NBLOCK = 0
WAT = {}
for _g in GROUPS[:-1]:
    for _n in _g:
        WAT[_n] = NBLOCK
        NBLOCK += WIDE.get(_n, DC)
WAT["qk2"], WAT["vo2"] = NBLOCK, NBLOCK + DC
NBLOCK += 2 * DC

SCALED = [0, 1, 3, 6, 7]
COLS = ["ln1_g", "ln1_b", "ln2_g", "ln2_b", "bq0", "bk0", "bv0", "bq1", "bk1", "bv1",
        "bd", "bri", "brh", "bzi", "bzh", "bni", "bnh", "b1"]
CAT = {n: DC * j for j, n in enumerate(COLS)}
NCOL = DC * (len(COLS) - 1) + FF // P
ROWV = ["bo0", "b2", "bo1", "bo2", "g1", "be1", "g2", "be2", "g3", "be3"]
RAT = {n: j for j, n in enumerate(ROWV)}
BAT = {"q0": 0, "k0": 2, "v0": 4, "q1": 6, "r": 8, "z": 10, "nh": 12, "b1": 14}



def attention(s, a):
    steps = []
    for t in range(H + 2):
        if t < H:
            steps.append(("score", s, a, t))
        if 1 <= t <= H:
            steps.append(("turn_p", s, a, t - 1))
        if t >= 2:
            steps.append(("pv", s, a, t - 2))
    return steps + [("heads", s, a)]


def before(s):
    return [("prep", s), ("stats", s, "in"), "*", "*", ("norm", s, "in"), ("residual", s, "in"), "*",
            ("turn", s, "norm"), "*", ("qk", s, 0), ("v", s, 0)]


def middle(s):
    out = ["*", "*", ("turn", s, "heads"), "*", "*", ("proj", s, "o0"), ("residual", s, "mid"),
           ("stats", s, "mid"), "*", "*", "*", "*", ("norm", s, "mid"), "*", ("turn", s, "norm"), "*", "*"]
    for j in range(UPS + 2):
        if j < UPS:
            out.append(("up", s, j))
        if j >= 2:
            out.append(("down", s, j - 2))
        out.append("*")
    return out + [("mlp_sum", s), "*", "*", ("turn", s, "sum"), ("residual", s, "x2"), "*", "*", ("qk", s, 1), ("v", s, 1)]


def late(s):
    return [("turn", s, "heads"), "*", "*", ("proj", s, "o1"), ("stats", s, "l1"), ("centre", s, "l1"),
            ("turn_adj", s), "*", "*", "*", ("norm", s, "l1"), ("residual", s, "l1"), "*",
            ("turn", s, "norm"), "*", "*", ("a2", s), "*", "*", ("score2", s), "*", "*", ("turn_p2", s), "*", "*",
            ("z2", s), "*", ("turn", s, "z2"), "*", "*", ("proj", s, "vo2"),
            ("stats", s, "l2"), ("centre", s, "l2"), "*", ("masks", s, 0), ("count", s, 0), "*",
            ("norm", s, "l2"), ("hidden", s), ("turn", s, "norm"), "*", "*",
            ("agg", s, 0), ("agg", s, 1), ("masks", s, 1), ("wd", s, 0), ("count", s, 1), ("agg", s, 2),
            ("wd", s, 1), ("agg", s, 3), ("wd", s, 2), ("wd", s, 3), ("relu", s), ("gates_hid", s), "*", ("gates_out", s), ("gates", s)]


def slot(att, lin):
    att, out = list(att), []
    for step in lin:
        if step != "*":
            out.append(step)
        elif att:
            out.append(att.pop(0))
    return out + att


def tail(s):
    return [("turn_back", s), ("stats", s, "fin"), ("centre", s, "fin"), ("norm", s, "fin"), ("store", s)]


def finish(s, nxt):
    if nxt:
        return late(s) + [("load", s, 1)] + ["*"] + tail(s) + before(s)
    return late(s) + tail(s)


PROLOGUE = [("load", 0, 0), ("load", 1, 0)] + slot([], before(0)) + slot(attention(0, 0), before(1))
BODY = (slot(attention(1, 0), middle(0)) + slot(attention(0, 1), middle(1))
        + slot(attention(1, 1), finish(0, True)) + slot(attention(0, 0), finish(1, True)))
EPILOGUE = (slot(attention(1, 0), middle(0)) + slot(attention(0, 1), middle(1))
            + slot(attention(1, 1), finish(0, False)) + slot([], finish(1, False)))


class Tally:

    def __init__(self, loops):
        self.loops, self.i, self.base, self.rate, self.here = loops, None, {}, {}, {}
        for step in BODY:
            self.rate[step[0]] = self.rate.get(step[0], 0) + 1
            self.rate[step[:2]] = self.rate.get(step[:2], 0) + 1

    def enter(self, step):
        for key in (step[0], step[:2]):
            self.here[key] = self.here.get(key, 0) + 1

    def loop_begins(self, i):
        self.base, self.here, self.i = self.here, {}, i

    def loop_ends(self):
        self.i = None
        keys = set(self.rate) | set(self.base)
        self.here = {k: self.base.get(k, 0) + self.loops * self.rate.get(k, 0) for k in keys}
        self.base = {}

    def value(self, key, per, less):
        n = per * (self.base.get(key, 0) + self.here.get(key, 0)) - less
        if self.i is None or not self.rate.get(key):
            return n
        return self.i * (per * self.rate[key]) + n


def build(nc, x, adj, weights, cols, rows, out):
    loops = x.shape[0] // 2 - 1
    x_v = x.rearrange("b (q p) d -> b p q d", p=P)
    adj_v = adj.rearrange("b (q p) k -> b p q k", p=P)
    out_v = out.rearrange("b (q p) d -> b p q d", p=P)

    with ExitStack() as ctx:
        def sb(name, shape, dt=F32):
            return ctx.enter_context(nc.sbuf_tensor(name, shape, dt))

        def sem(name):
            return ctx.enter_context(nc.semaphore(name))

        WH = sb("WH", [P, NBLOCK, D], F32R)
        WL = sb("WL", [P, NBLOCK, D], F32R)
        colv = sb("colv", [P, NCOL])
        rowv = sb("rowv", [P, len(ROWV), D])
        bias = sb("bias", [P, 14 + FF // P])
        halves = sb("halves", [P, 2 * DC])
        lneps = sb("lneps", [P, RT])
        power = sb("power", [P, RT])
        ident = sb("ident", [P, P])
        ones = sb("ones", [P, P])
        ones_r = sb("ones_r", [P, P], F32R)
        vb = sb("vb", [P, DC, P])
        xin = sb("xin", [P, 2, RT, D])
        adjb = sb("adjb", [P, 2, RT, D], I32)
        nb = sb("nb", [P, 2, 2, W])
        res = sb("res", [P, 2, RT, D])
        y = sb("y", [P, 2, RT, D])
        nx = sb("nx", [P, 2, RT, D])
        qh = sb("qh", [P, 2, DC, D], F32R)
        ql = sb("ql", [P, 2, DC, D], F32R)
        kh = sb("kh", [P, 2, DC, D], F32R)
        kl = sb("kl", [P, 2, DC, D], F32R)
        V = sb("V", [P, 2, RT, D])
        keep = sb("keep", [P, 2, RT])
        tTh = sb("tTh", [P, DC, D], F32R)
        tTl = sb("tTl", [P, DC, D], F32R)
        hf = sb("hf", [P, 2, W])
        hh = sb("hh", [P, 2, W], F32R)
        hl = sb("hl", [P, 2, W], F32R)
        rc = sb("rc", [P, 2, D])
        st = sb("st", [P, RT, 6])
        mv = sb("mv", [P, RT, 2])
        rstd = sb("rstd", [P, 2, RT])
        nmax2 = sb("nmax2", [P, RT])
        rsum2 = sb("rsum2", [P, RT])
        rec2 = sb("rec2", [P, RT])
        S = sb("S", [P, 2, RT, D])
        PT = sb("PT", [P, 2, DC, D])
        nmax = sb("nmax", [P, 2, RT])
        rsum = sb("rsum", [P, RT, H])
        rec = sb("rec", [P, RT, H])
        bank = ctx.enter_context(nc.psum_tensor("bank", [P, 8, W], F32))

        def halved(b):
            return bank[:, b, :].rearrange("p (c n) -> p c n", c=2)

        def flat(ap):
            return ap.rearrange("p a b -> p (a b)")

        def f32(ap):
            return ap.bitcast(F32)

        stage = nb[:, :, :, :].rearrange("p a b c -> p (a b c)")
        nbias = [[nb[:, s, a, :].rearrange("p (r k) -> p r k", r=RT) for a in range(2)] for s in range(2)]
        adjf = [f32(adjb[:, s, :, :]) for s in range(2)]
        adjT = [nbias[s][0] for s in range(2)]
        mask = [[qh[:, s, :, :], ql[:, s, :, :]] for s in range(2)]
        hidh = [kh[:, s, :, :] for s in range(2)]
        hidl = [kl[:, s, :, :] for s in range(2)]

        def wt(half, name, c, lo, hi):
            n = FF // D if name == "w1" else 1
            a = WAT[name] + c * n
            return half[:, a:a + n, :].rearrange("p b d -> p (b d)")[:, lo:hi]

        def col(name, c=0):
            return colv[:, CAT[name] + c:CAT[name] + c + 1]

        def bcol(name, c=0):
            return bias[:, BAT[name] + c:BAT[name] + c + 1]

        def row(name):
            return rowv[:, RAT[name], :]

        s_ident0, s_ident, s_const = sem("s_ident0"), sem("s_ident"), sem("s_const")
        waited = sem("waited")
        s_vecs, s_staged = sem("s_vecs"), sem("s_staged")
        s_fold, s_bias, s_scaled = sem("s_fold"), sem("s_bias"), sem("s_scaled")
        s_whi, s_wlo, s_prod, s_vb, s_rowfix = sem("s_whi"), sem("s_wlo"), sem("s_prod"), sem("s_vb"), sem("s_rowfix")
        x_in = [sem("x_in0"), sem("x_in1")]
        adj_in = [sem("adj_in0"), sem("adj_in1")]
        stored = [sem("stored0"), sem("stored1")]
        prepped = sem("prepped")
        stat_ok = sem("stat_ok")
        mean_ok = sem("mean_ok")
        var_ok = sem("var_ok")
        rstd_ok = sem("rstd_ok")
        cent_ok = sem("cent_ok")
        norm_ok = sem("norm_ok")
        res_ok = sem("res_ok")
        turn_mm = sem("turn_mm")
        turn_hi, turn_lo = sem("turn_hi"), sem("turn_lo")
        qk_mm = sem("qk_mm")
        qk_hi, qk_lo = sem("qk_hi"), sem("qk_lo")
        v_mm, v_ok = sem("v_mm"), sem("v_ok")
        score_mm = sem("score_mm")
        score_max = sem("score_max")
        prob_ok = sem("prob_ok")
        turn_p_mm, turn_p_ok = sem("turn_p_mm"), sem("turn_p_ok")
        pv_mm = sem("pv_mm")
        rec_ok, heads_ok = sem("rec_ok"), sem("heads_ok")
        proj_mm, proj_ok = sem("proj_mm"), sem("proj_ok")
        up_mm = sem("up_mm")
        up_act = sem("up_act")
        up_hi, up_lo = sem("up_hi"), sem("up_lo")
        down_mm, sum_ok = sem("down_mm"), sem("sum_ok")
        a2_mm, a2_hi, a2_lo = sem("a2_mm"), sem("a2_hi"), sem("a2_lo")
        score2_mm = sem("score2_mm")
        score2_max, prob2_ok = sem("score2_max"), sem("prob2_ok")
        turn_p2_mm, turn_p2_ok = sem("turn_p2_mm"), sem("turn_p2_ok")
        z2_mm, rec2_ok, z2_ok = sem("z2_mm"), sem("rec2_ok"), sem("z2_ok")
        hid_hi, hid_lo = sem("hid_hi"), sem("hid_lo")
        adjT_mm, adjT_ok = sem("adjT_mm"), sem("adjT_ok")
        mask_ok = sem("mask_ok")
        cnt_mm, cnt_eps, rc_ok = sem("cnt_mm"), sem("cnt_eps"), sem("rc_ok")
        agg_mm, agg_ok, agg_hi, agg_lo = sem("agg_mm"), sem("agg_ok"), sem("agg_hi"), sem("agg_lo")
        wd_mm = sem("wd_mm")
        relu_ok = sem("relu_ok")
        relu_hi, relu_lo = sem("relu_hi"), sem("relu_lo")
        hid_mm, out_mm = sem("hid_mm"), sem("out_mm")
        gate_act = sem("gate_act")
        pre_ok = sem("pre_ok")
        cand_ok = sem("cand_ok")
        mix_ok = sem("mix_ok")
        back_mm = sem("back_mm")

        block = ctx.enter_context(nc.Block())

        def walk(e, tally, ops):
            def run(steps):
                for step in steps:
                    tally.enter(step)
                    if step[0] in ops:
                        ops[step[0]](*step[1:])

            run(PROLOGUE)
            with e.Fori(0, loops) as i:
                tally.loop_begins(i)
                run(BODY)
            tally.loop_ends()
            run(EPILOGUE)

        def waiter(e, tally):
            def wait(s, key, per=1, less=0, alone=False):
                ins = e.wait_ge(s, tally.value(key, per, less))
                if alone:
                    ins.then_inc(waited, 1)
            return wait

        def group_span(j):
            return WAT[GROUPS[j][0]], sum(WIDE.get(n, DC) for n in GROUPS[j])

        @block.sync
        def _(e):
            t = Tally(loops)
            wait = waiter(e, t)
            e.dma_start(colv[:, :], cols).then_inc(s_vecs, 16)
            e.dma_start(rowv[:, :, :], rows).then_inc(s_vecs, 16)
            at = 0
            for j, names in enumerate(GROUPS):
                n = sum(WIDE.get(m, DC) for m in names) * D
                if j >= 1:
                    e.wait_ge(s_wlo, j)
                e.dma_start(stage[:, 0:n], weights[:, at:at + n]).then_inc(s_staged, 16)
                at += n

            def load(s, ahead):
                g = s if t.i is None else t.i * 2 + (2 * ahead + s)
                if ahead:
                    wait(turn_hi, "turn", alone=True)
                    wait(res_ok, "residual", alone=True)
                    wait(adjT_mm, "turn_adj", alone=True)
                e.dma_start(xin[:, s, :, :], x_v[bass.ds(g, 1), :, :, :].rearrange("a p r d -> (a p) r d")).then_inc(x_in[s], 16)
                e.dma_start(adjb[:, s, :, :], adj_v[bass.ds(g, 1), :, :, :].rearrange("a p r d -> (a p) r d")).then_inc(adj_in[s], 16)

            def store(s):
                g = 2 * loops + s if t.i is None else t.i * 2 + s
                wait(norm_ok, "norm", 2, alone=True)
                e.dma_start(out_v[bass.ds(g, 1), :, :, :].rearrange("a p r d -> (a p) r d"), y[:, s, :, :]).then_inc(stored[s], 16)

            walk(e, t, {"load": load, "store": store})
            for s in range(2):
                wait(stored[s], ("store", s), 16)

        @block.gpsimd
        def _(e):
            t = Tally(loops)
            wait = waiter(e, t)
            e.memset(ident[:, :], 0.0).then_inc(s_ident0, 1)
            e.memset(lneps[:, :], LN_EPS).then_inc(s_const, 1)
            e.memset(power[:, :], -0.5).then_inc(s_const, 1)
            e.memset(ones[:, :], 1.0).then_inc(s_const, 1)
            e.wait_ge(s_ident0, 1)
            e.affine_select(out=ident[:, :], in_=ident[:, :], compare_op=ALU.not_equal, fill=1.0,
                            base=0, pattern=[[-1, P]], channel_multiplier=1).then_inc(s_ident, 1)
            e.wait_ge(s_const, 3)
            e.wait_ge(s_rowfix, 2)

            def stats(s, which):
                wait(mean_ok, "stats", 2)
                e.tensor_tensor(rstd[:, s, :], mv[:, :, 1], lneps[:, :], ALU.add).then_inc(var_ok, 1)
                wait(var_ok, "stats")
                e.tensor_tensor(rstd[:, s, :], rstd[:, s, :], power[:, :], ALU.pow).then_inc(rstd_ok, 1)

            def residual(s, which):
                src, name = {"in": (xin, "bo0"), "mid": (y, "b2"), "x2": (y, "bo1"), "l1": (nx, "bo2")}[which]
                if which == "in":
                    wait(x_in[s], ("load", s), 16)
                    if t.i is not None:
                        wait(mix_ok, "gates", 4)
                elif which == "mid":
                    wait(proj_ok, "proj")
                elif which == "x2":
                    wait(sum_ok, "mlp_sum")
                else:
                    wait(norm_ok, "norm", 2)
                for r in range(RT):
                    op = e.tensor_tensor(res[:, s, r, :], src[:, s, r, :], row(name), ALU.add)
                op.then_inc(res_ok, 1)

            def high(slot, done):
                e.tensor_scalar(hh[:, slot, :], hf[:, slot, :], 1.0, 0.0, ALU.mult, ALU.add).then_inc(done, 1)

            def low(slot, done):
                e.tensor_tensor(hl[:, slot, :], hf[:, slot, :], f32(hh[:, slot, :]), ALU.subtract).then_inc(done, 1)

            def up(s, j):
                if j >= 2:
                    wait(down_mm, "down", 1, -1)
                wait(up_act, "up", 2, alone=True)
                high(j % 2, up_hi)
                wait(up_hi, "up")
                low(j % 2, up_lo)

            def hidden(s):
                wait(norm_ok, "norm", 2, alone=True)
                e.tensor_scalar(flat(hidh[s]), flat(nx[:, s, :, :]), 1.0, 0.0, ALU.mult, ALU.add).then_inc(hid_hi, 1)

            def agg(s, d):
                if d >= 2:
                    wait(wd_mm, "wd")
                wait(agg_ok, "agg", alone=True)
                high(d % 2, agg_hi)
                wait(agg_hi, "agg")
                low(d % 2, agg_lo)

            def relu(s):
                wait(relu_ok, "relu", 2, alone=True)
                high(0, relu_hi)

            walk(e, t, {"stats": stats, "residual": residual, "up": up, "hidden": hidden, "agg": agg,
                        "relu": relu})

        @block.scalar
        def _(e):
            t = Tally(loops)
            wait = waiter(e, t)
            for j in range(len(GROUPS) - 1):
                a, n = group_span(j)
                e.wait_ge(s_staged, 16 * (j + 1))
                if j in SCALED:
                    e.wait_ge(s_scaled, SCALED.index(j) + 1)
                e.activation(flat(WH[:, a:a + n, :]), stage[:, 0:n * D], ACT.Copy).then_inc(s_whi, 1)
            for j, name in enumerate(("qk2", "vo2")):
                e.wait_ge(s_prod, j + 1)
                e.activation(flat(WH[:, WAT[name]:WAT[name] + DC, :]), bank[:, 4 + j, :], ACT.Copy).then_inc(s_whi, 1)

            def copy(dst, src, done):
                e.activation(dst, src, ACT.Copy).then_inc(done, 1)

            def turn(s, src):
                wait(turn_mm, "turn")
                copy(flat(tTh[:, :, :]), bank[:, 4, :], turn_hi)

            def qk(s, a):
                for n, (dst, b) in enumerate(((qh, 5), (kh, 6))):
                    wait(qk_mm, "qk", 2, 1 - n)
                    for m in range(DC):
                        bc = bcol("q%d" % a, m) if n == 0 else (bcol("k0", m) if a == 0 else col("bk1", m))
                        e.activation(dst[:, s, m, :], halved(b)[:, m, :], ACT.Identity, bias=bc).then_inc(qk_hi, 1)

            def v(s, a):
                wait(v_mm, "v")
                copy(flat(V[:, s, :, :]), bank[:, 7, :], v_ok)

            def score(s, a, h):
                for r in range(RT):
                    wait(score_max, "score", 2, 1 - r)
                    e.activation(S[:, h % 2, r, :], S[:, h % 2, r, :], ACT.Exp, bias=nmax[:, h % 2, r:r + 1],
                                 scale=-1.0, accum_out=rsum[:, r, h:h + 1]).then_inc(prob_ok, 1)

            def turn_p(s, a, h):
                wait(turn_p_mm, "turn_p")
                if h >= 2:
                    wait(pv_mm, "pv")
                copy(flat(PT[:, h % 2, :, :]), bank[:, 2, :], turn_p_ok)

            def up(s, j):
                wait(up_mm, "up")
                if j >= 2:
                    wait(up_lo, "up", 1, 2)
                for f in range(2):
                    e.activation(hf[:, j % 2, f * D:f * D + D], halved(6 + j % 2)[:, f, :], ACT.Gelu,
                                 bias=bcol("b1", 2 * j + f)).then_inc(up_act, 1)

            def a2(s):
                wait(a2_mm, "a2")
                copy(flat(qh[:, s, :, :]), bank[:, 5, :], a2_hi)

            def score2(s):
                for r in range(RT):
                    wait(score2_max, "score2", 2, 1 - r)
                    e.activation(hf[:, 0, r * D:r * D + D], hf[:, 0, r * D:r * D + D], ACT.Exp, bias=nmax2[:, r:r + 1],
                                 scale=-1.0, accum_out=rsum2[:, r:r + 1]).then_inc(prob2_ok, 1)

            def turn_p2(s):
                wait(turn_p2_mm, "turn_p2")
                copy(hf[:, 1, :], bank[:, 7, :], turn_p2_ok)

            def turn_adj(s):
                wait(adjT_mm, "turn_adj")
                copy(flat(adjT[s]), bank[:, 7, :], adjT_ok)

            def relu(s):
                wait(wd_mm, "wd")
                for m in range(DC):
                    e.activation(hf[:, 0, m * D:m * D + D], halved(4)[:, m, :], ACT.Relu, bias=col("bd", m)).then_inc(relu_ok, 1)

            def gates(s):
                wait(out_mm, "gates_out")
                for b, name, dst in ((5, "r", hf[:, 1, :]), (6, "z", flat(V[:, s, :, :]))):
                    for m in range(DC):
                        e.activation(dst[:, m * D:m * D + D], halved(b)[:, m, :], ACT.Tanh, bias=bcol(name, m),
                                     scale=0.5).then_inc(gate_act, 1)
                for m in range(DC):
                    e.activation(res[:, s, m, :], halved(7)[:, m, :], ACT.Identity, bias=bcol("nh", m)).then_inc(gate_act, 1)
                wait(pre_ok, "gates", 2)
                for m in range(DC):
                    e.activation(res[:, s, m, :], hf[:, 1, m * D:m * D + D], ACT.Tanh, bias=col("bni", m)).then_inc(cand_ok, 1)

            walk(e, t, {"turn": turn, "qk": qk, "v": v, "score": score, "turn_p": turn_p, "up": up, "a2": a2,
                        "score2": score2, "turn_p2": turn_p2, "turn_adj": turn_adj, "relu": relu,
                        "gates": gates})

        @block.vector
        def _(e):
            t = Tally(loops)
            wait = waiter(e, t)
            tsc, tt, stt = e.tensor_scalar, e.tensor_tensor, e.scalar_tensor_tensor
            e.wait_ge(s_vecs, 32)
            e.wait_ge(s_const, 3)
            tt(halves[:, 0:DC], colv[:, CAT["bri"]:CAT["bri"] + DC], colv[:, CAT["brh"]:CAT["brh"] + DC], ALU.add).then_inc(s_bias, 1)
            tt(halves[:, DC:2 * DC], colv[:, CAT["bzi"]:CAT["bzi"] + DC], colv[:, CAT["bzh"]:CAT["bzh"] + DC], ALU.add).then_inc(s_bias, 1)
            e.wait_ge(s_bias, 2)
            tsc(bias[:, BAT["r"]:BAT["r"] + 2 * DC], halves[:, :], 0.5, None, ALU.mult).then_inc(s_bias, 1)
            tsc(bias[:, BAT["nh"]:BAT["nh"] + DC], colv[:, CAT["bnh"]:CAT["bnh"] + DC], 0.5, None, ALU.mult).then_inc(s_bias, 1)
            tsc(bias[:, BAT["q1"]:BAT["q1"] + DC], colv[:, CAT["bq1"]:CAT["bq1"] + DC], -QSCALE, None, ALU.mult).then_inc(s_bias, 1)
            tsc(ones_r[:, :], ones[:, :], 1.0, None, ALU.mult).then_inc(s_bias, 1)

            def spread(src, n):
                for c in range(DC):
                    tsc(vb[:, c, :], ones[:, :], src(c), None, ALU.mult).then_inc(s_vb, 1)

            def scale(lo, n, by, const):
                part = stage[:, lo:lo + n]
                if by is None:
                    return tsc(part, part, const, None, ALU.mult)
                return tsc(part, part, by, const, ALU.mult, ALU.mult)

            def split_low(j, a, n, src):
                e.wait_ge(s_whi, j + 1)
                tt(flat(WL[:, a:a + n, :]), src, f32(flat(WH[:, a:a + n, :])), ALU.subtract).then_inc(s_wlo, 1)

            for j in range(len(GROUPS)):
                e.wait_ge(s_staged, 16 * (j + 1))
                if j == 0:
                    e.wait_ge(s_fold, 1)
                    for n, name in enumerate(("q0", "k0", "v0")):
                        tt(bias[:, BAT[name]:BAT[name] + DC], bank[:, 4, DC * n:DC * n + DC],
                           colv[:, CAT["b" + name]:CAT["b" + name] + DC], ALU.add).then_inc(s_bias, 1)
                    e.wait_ge(s_bias, 9)
                    tsc(bias[:, BAT["q0"]:BAT["q0"] + DC], bias[:, BAT["q0"]:BAT["q0"] + DC], -QSCALE, None, ALU.mult).then_inc(s_bias, 1)
                    spread(lambda c: bcol("v0", c), 0)
                    e.wait_ge(s_fold, 2)
                    tt(row("bo0"), bank[:, 5, 0:D], row("bo0"), ALU.add).then_inc(s_rowfix, 1)
                    for w, const in enumerate((-QSCALE, 1.0, 1.0)):
                        for c in range(DC):
                            ins = scale((DC * w + c) * D, D, col("ln1_g", c), const)
                    ins.then_inc(s_scaled, 1)
                elif j == 1:
                    e.wait_ge(s_fold, 3)
                    tt(bias[:, BAT["b1"]:BAT["b1"] + FF // P], bank[:, 6, 0:FF // P],
                       colv[:, CAT["b1"]:CAT["b1"] + FF // P], ALU.add).then_inc(s_bias, 1)
                    for c in range(DC):
                        ins = scale(c * FF, FF, col("ln2_g", c), 1.0)
                    ins.then_inc(s_scaled, 1)
                elif j == 3:
                    spread(lambda c: col("bv1", c), 1)
                    e.wait_ge(s_fold, 4)
                    tt(row("bo1"), bank[:, 7, 0:D], row("bo1"), ALU.add).then_inc(s_rowfix, 1)
                    scale(0, DC * D, None, -QSCALE).then_inc(s_scaled, 1)
                elif j == 6:
                    scale(DC * D, DC * D, None, 0.5).then_inc(s_scaled, 1)
                elif j == 7:
                    scale(0, DC * D, None, -1.0 / float(np.sqrt(D))).then_inc(s_scaled, 1)
                if j < len(GROUPS) - 1:
                    a, n = group_span(j)
                    split_low(j, a, n, stage[:, 0:n * D])
            for n, name in enumerate(("qk2", "vo2")):
                split_low(len(GROUPS) - 1 + n, WAT[name], DC, bank[:, 4 + n, :])

            def source(s, which):
                return halved(5) if which == "fin" else (xin if which == "in" else y)[:, s, :, :]

            def prep(s):
                f, n0, n1 = flat(adjf[s]), nb[:, s, 0, :], nb[:, s, 1, :]
                wait(adj_in[s], ("load", s), 16)
                e.tensor_copy(f, flat(adjb[:, s, :, :])).then_inc(prepped, 1)
                wait(prepped, "prep", 7, 6)
                stt(n0, f, -0.1, f, ALU.mult, ALU.mult).then_inc(prepped, 1)
                tsc(n1, f, 0.0, BIG, ALU.is_le, ALU.mult).then_inc(prepped, 1)
                wait(prepped, "prep", 7, 4)
                tt(n0, n0, n1, ALU.add).then_inc(prepped, 1)
                wait(prepped, "prep", 7, 3)
                tsc(n1, f, 0.0, BIG, ALU.is_equal, ALU.mult).then_inc(prepped, 1)
                wait(prepped, "prep", 7, 2)
                e.tensor_reduce(keep[:, s, :], nbias[s][1], mybir.AxisListType.X, ALU.min).then_inc(prepped, 1)
                wait(prepped, "prep", 7, 1)
                tsc(keep[:, s, :], keep[:, s, :], 1.0, None, ALU.is_lt).then_inc(prepped, 1)

            def stats(s, which):
                src = source(s, which)
                if which == "in":
                    wait(x_in[s], ("load", s), 16)
                elif which == "fin":
                    wait(back_mm, "turn_back")
                else:
                    wait(proj_ok, "proj")
                for r in range(RT):
                    e.bn_stats(st[:, r, :], src[:, r, :]).then_inc(stat_ok, 1)
                for r in range(RT):
                    wait(stat_ok, "stats", 2, 1 - r, alone=True)
                    e.bn_aggr(mv[:, r, :], st[:, r, :]).then_inc(mean_ok, 1)

            def gains(which):
                n = {"l1": "1", "l2": "2", "fin": "3"}[which]
                return row("g" + n), row("be" + n)

            def centre(s, which):
                src, dst = source(s, which), (y if which == "fin" else nx)
                for r in range(RT):
                    wait(mean_ok, "stats", 2, 1 - r)
                    stt(dst[:, s, r, :], src[:, r, :], mv[:, r, 0:1], gains(which)[0], ALU.subtract, ALU.mult).then_inc(cent_ok, 1)

            def norm(s, which):
                wait(rstd_ok, "stats")
                if which == "in" and t.i is not None:
                    wait(stored[s], ("store", s), 16)
                for r in range(RT):
                    if which in ("in", "mid"):
                        tsc(nx[:, s, r, :], source(s, which)[:, r, :], mv[:, r, 0:1], rstd[:, s, r:r + 1],
                            ALU.subtract, ALU.mult).then_inc(norm_ok, 1)
                    else:
                        dst = (y if which == "fin" else nx)[:, s, r, :]
                        wait(cent_ok, "centre", 2, 1 - r)
                        stt(dst, dst, rstd[:, s, r:r + 1], gains(which)[1], ALU.mult, ALU.add).then_inc(norm_ok, 1)

            def turn(s, src):
                wait(turn_hi, "turn")
                tt(flat(tTl[:, :, :]), bank[:, 4, :], f32(flat(tTh[:, :, :])), ALU.subtract).then_inc(turn_lo, 1)

            def qk(s, a):
                for n, (hi, lo, b) in enumerate(((qh, ql, 5), (kh, kl, 6))):
                    wait(qk_hi, "qk", 4, 2 - 2 * n)
                    for m in range(DC):
                        bc = bcol("q%d" % a, m) if n == 0 else (bcol("k0", m) if a == 0 else col("bk1", m))
                        stt(lo[:, s, m, :], halved(b)[:, m, :], bc, f32(hi[:, s, m, :]), ALU.add, ALU.subtract).then_inc(qk_lo, 1)

            def score(s, a, h):
                if h >= 2:
                    wait(turn_p_mm, "turn_p")
                wait(score_mm, "score", alone=True)
                for r in range(RT):
                    e.tensor_tensor_reduce(S[:, h % 2, r, :], halved(h % 2)[:, r, :], nbias[s][a][:, r, :], 1.0, 3.3e38,
                                           ALU.add, ALU.min, nmax[:, h % 2, r:r + 1]).then_inc(score_max, 1)

            def heads(s, a):
                wait(pv_mm, "pv")
                e.reciprocal(flat(rec[:, :, :]), flat(rsum[:, :, :])).then_inc(rec_ok, 1)
                wait(rec_ok, "heads")
                tt(flat(nx[:, s, :, :]).rearrange("p (n e) -> p n e", e=HD),
                   bank[:, 3, :].rearrange("p (n e) -> p n e", e=HD),
                   flat(rec[:, :, :]).unsqueeze(2).to_broadcast([P, RT * H, HD]), ALU.mult).then_inc(heads_ok, 1)

            def proj(s, name):
                wait(proj_mm, "proj")
                wait(res_ok, "residual")
                tt(flat(y[:, s, :, :]), bank[:, 5, :], flat(res[:, s, :, :]), ALU.add).then_inc(proj_ok, 1)

            def mlp_sum(s):
                wait(down_mm, "down")
                wait(res_ok, "residual")
                tt(flat(y[:, s, :, :]), bank[:, 5, :], flat(res[:, s, :, :]), ALU.add).then_inc(sum_ok, 1)

            def a2(s):
                wait(a2_hi, "a2")
                tt(flat(ql[:, s, :, :]), bank[:, 5, :], f32(flat(qh[:, s, :, :])), ALU.subtract).then_inc(a2_lo, 1)

            def score2(s):
                wait(score2_mm, "score2", alone=True)
                for r in range(RT):
                    e.tensor_tensor_reduce(hf[:, 0, r * D:r * D + D], halved(6)[:, r, :], nbias[s][1][:, r, :],
                                           keep[:, s, r:r + 1], 3.3e38, ALU.add, ALU.min, nmax2[:, r:r + 1]).then_inc(score2_max, 1)

            def z2(s):
                wait(z2_mm, "z2")
                e.reciprocal(rec2[:, :], rsum2[:, :]).then_inc(rec2_ok, 1)
                wait(rec2_ok, "z2")
                for r in range(RT):
                    tsc(y[:, s, r, :], halved(5)[:, r, :], rec2[:, r:r + 1], None, ALU.mult).then_inc(z2_ok, 1)

            def hidden(s):
                wait(hid_hi, "hidden")
                tt(flat(hidl[s]), flat(nx[:, s, :, :]), f32(flat(hidh[s])), ALU.subtract).then_inc(hid_lo, 1)

            def masks(s, p):
                wait(adjT_ok, "turn_adj")
                if p:
                    wait(agg_mm, "agg")
                for l in range(2):
                    tsc(flat(mask[s][l]), flat(adjT[s]), float(2 * p + l + 1), None, ALU.is_equal).then_inc(mask_ok, 1)

            def count(s, p):
                wait(cnt_mm, "count")
                tsc(flat(rc[:, :, :]), bank[:, 5, :], AGG_EPS, None, ALU.add).then_inc(cnt_eps, 1)
                wait(cnt_eps, "count")
                e.reciprocal(flat(rc[:, :, :]), flat(rc[:, :, :])).then_inc(rc_ok, 1)

            def agg(s, d):
                wait(agg_mm, "agg")
                wait(rc_ok, "count")
                if d >= 2:
                    wait(agg_lo, "agg", 1, 2)
                tt(hf[:, d % 2, :].rearrange("p (c m) -> p c m", c=DC), halved(6 + d % 2),
                   rc[:, d % 2, :].unsqueeze(1).to_broadcast([P, DC, D]), ALU.mult).then_inc(agg_ok, 1)

            def relu(s):
                wait(relu_hi, "relu")
                tt(hl[:, 0, :], hf[:, 0, :], f32(hh[:, 0, :]), ALU.subtract).then_inc(relu_lo, 1)

            def gates(s):
                r, z, n = hf[:, 1, :], flat(V[:, s, :, :]), flat(res[:, s, :, :])
                wait(gate_act, "gates", 6)
                stt(r, r, 1.0, n, ALU.add, ALU.mult).then_inc(pre_ok, 1)
                wait(pre_ok, "gates", 2, 1)
                tt(r, bank[:, 4, :], r, ALU.add).then_inc(pre_ok, 1)
                wait(cand_ok, "gates", 2)
                tt(r, f32(flat(tTh[:, :, :])), n, ALU.subtract).then_inc(mix_ok, 1)
                wait(mix_ok, "gates", 4, 3)
                tt(r, r, f32(flat(tTl[:, :, :])), ALU.add).then_inc(mix_ok, 1)
                wait(mix_ok, "gates", 4, 2)
                stt(r, z, 1.0, r, ALU.add, ALU.mult).then_inc(mix_ok, 1)
                wait(mix_ok, "gates", 4, 1)
                stt(flat(y[:, s, :, :]), r, 0.5, n, ALU.mult, ALU.add).then_inc(mix_ok, 1)

            walk(e, t, {"prep": prep, "stats": stats, "centre": centre, "norm": norm, "turn": turn, "qk": qk,
                        "score": score, "heads": heads, "proj": proj, "mlp_sum": mlp_sum, "a2": a2, "score2": score2,
                        "z2": z2, "hidden": hidden, "masks": masks, "count": count, "agg": agg, "relu": relu,
                        "gates": gates})

        @block.tensor
        def _(e):
            t = Tally(loops)
            wait = waiter(e, t)

            def mm3(dst, left, right, first=True, last=True, shared=False):
                (lh, ll), (rh, rl) = left, right
                e.matmul(dst, lh, rh, start=first, stop=False, skip_group_check=shared)
                e.matmul(dst, lh, rl, start=False, stop=False, skip_group_check=shared)
                return e.matmul(dst, ll, rh, start=False, stop=last, skip_group_check=shared)

            def w2(name, c, lo, n):
                return wt(WH, name, c, lo, lo + n), wt(WL, name, c, lo, lo + n)

            def tT(c, lo=0, n=D):
                return tTh[:, c, lo:lo + n], tTl[:, c, lo:lo + n]

            def by_feature(b, name, m, done=None, first=True, last=True, shared=False):
                for c in range(DC):
                    ins = mm3(halved(b)[:, m, :], w2(name, c, m * P, P), tT(c), first and c == 0,
                              last and c == DC - 1, shared)
                return ins

            def by_row(b, name):
                for r in range(RT):
                    for c in range(DC):
                        ins = mm3(halved(b)[:, r, :], tT(c, r * P, P), w2(name, c, 0, D), c == 0, c == DC - 1)
                return ins

            def staged(block, c, lo, n, width=D):
                a = block * D + c * width + lo
                return stage[:, a:a + n]

            e.wait_ge(s_vecs, 32)
            e.wait_ge(s_staged, 16)
            for n in range(3):
                for m in range(DC):
                    for c in range(DC):
                        ins = e.matmul(bank[:, 4, DC * n + m:DC * n + m + 1], staged(DC * n, c, m * P, P), col("ln1_b", c),
                                       start=c == 0, stop=c == DC - 1)
            ins.then_inc(s_fold, 1)
            e.wait_ge(s_vb, DC)
            for c in range(DC):
                ins = e.matmul(bank[:, 5, 0:D], vb[:, c, :], staged(3 * DC, c, 0, D), start=c == 0, stop=c == DC - 1)
            ins.then_inc(s_fold, 1)
            e.wait_ge(s_staged, 32)
            for f in range(FF // P):
                for c in range(DC):
                    ins = e.matmul(bank[:, 6, f:f + 1], staged(0, c, f * P, P, FF), col("ln2_b", c),
                                   start=c == 0, stop=c == DC - 1)
            ins.then_inc(s_fold, 1)
            e.wait_ge(s_staged, 64)
            e.wait_ge(s_vb, 2 * DC)
            for c in range(DC):
                ins = e.matmul(bank[:, 7, 0:D], vb[:, c, :], staged(3 * DC, c, 0, D), start=c == 0, stop=c == DC - 1)
            ins.then_inc(s_fold, 1)
            e.wait_ge(s_staged, 16 * len(GROUPS))
            e.wait_ge(s_scaled, len(SCALED))
            for n in range(2):
                for m in range(DC):
                    for c in range(DC):
                        ins = e.matmul(halved(4 + n)[:, m, :], staged(2 * DC * n, c, m * P, P), staged(2 * DC * n + DC, c, 0, D),
                                       start=c == 0, stop=c == DC - 1)
                ins.then_inc(s_prod, 1)
            e.wait_ge(s_wlo, len(GROUPS) + 1)
            e.wait_ge(s_ident, 1)

            def turn(s, src):
                rows = y if src in ("sum", "z2") else nx
                if src == "heads":
                    wait(heads_ok, "heads")
                elif src == "norm":
                    wait(norm_ok, "norm", 2)
                elif src == "sum":
                    wait(sum_ok, "mlp_sum")
                else:
                    wait(z2_ok, "z2", 2)
                for c in range(DC):
                    for r in range(RT):
                        ins = e.transpose(halved(4)[:, c, r * P:r * P + P], rows[:, s, r, c * P:c * P + P], ident[:, :])
                ins.then_inc(turn_mm, 1)

            def qk(s, a):
                wait(turn_lo, "turn")
                for b, name in ((5, "q%d" % a), (6, "k%d" % a)):
                    for m in range(DC):
                        ins = by_feature(b, name, m)
                    ins.then_inc(qk_mm, 1)

            def v(s, a):
                by_row(7, "v%d" % a).then_inc(v_mm, 1)

            def score(s, a, h):
                c, p = h // HPC, h % HPC * HD
                if h == 0:
                    wait(qk_lo, "qk", 4)
                if h >= 2:
                    wait(score_max, "score", 2, 4)
                for r in range(RT):
                    ins = mm3(halved(h % 2)[:, r, :],
                              (qh[p:p + HD, s, c, r * P:r * P + P], ql[p:p + HD, s, c, r * P:r * P + P]),
                              (kh[p:p + HD, s, c, :], kl[p:p + HD, s, c, :]))
                ins.then_inc(score_mm, 1)

            def turn_p(s, a, h):
                wait(prob_ok, "score", 2, 2 if h + 1 < H else 0)
                if h >= 1:
                    wait(turn_p_ok, "turn_p", 1, 1)
                for k in range(DC):
                    for r in range(RT):
                        ins = e.transpose(halved(2)[:, k, r * P:r * P + P], S[:, h % 2, r, k * P:k * P + P], ident[:, :])
                ins.then_inc(turn_p_mm, 1)

            def pv(s, a, h):
                if h == 0:
                    wait(v_ok, "v")
                wait(turn_p_ok, "turn_p", 1, 1 if h + 1 < H else 0)
                for r in range(RT):
                    for k in range(DC):
                        ins = e.matmul(halved(3)[:, r, h * HD:h * HD + HD], PT[:, h % 2, k, r * P:r * P + P],
                                       V[:, s, k, h * HD:h * HD + HD], start=k == 0, stop=k == DC - 1)
                ins.then_inc(pv_mm, 1)

            def proj(s, name):
                wait(turn_lo, "turn")
                by_row(5, name).then_inc(proj_mm, 1)

            def up(s, j):
                wait(turn_lo, "turn")
                if j >= 2:
                    wait(up_act, "up", 2, 4)
                for f in range(2):
                    for c in range(DC):
                        ins = mm3(halved(6 + j % 2)[:, f, :], w2("w1", c, (2 * j + f) * P, P), tT(c), c == 0, c == DC - 1)
                ins.then_inc(up_mm, 1)

            def down(s, j):
                wait(up_lo, "up", 1, min(j + 2, UPS - 1) - j)
                for f in range(2):
                    for r in range(RT):
                        at = f * D + r * P
                        ins = mm3(halved(5)[:, r, :], (hh[:, j % 2, at:at + P], hl[:, j % 2, at:at + P]),
                                  w2("w2", 2 * j + f, 0, D), (j, f, r) == (0, 0, 0), (j, f) == (UPS - 1, 1), True)
                ins.then_inc(down_mm, 1)

            def a2(s):
                wait(turn_lo, "turn")
                for m in range(DC):
                    ins = by_feature(5, "qk2", m)
                ins.then_inc(a2_mm, 1)

            def score2(s):
                wait(a2_lo, "a2")
                for r in range(RT):
                    for c in range(DC):
                        ins = mm3(halved(6)[:, r, :], (qh[:, s, c, r * P:r * P + P], ql[:, s, c, r * P:r * P + P]), tT(c),
                                  c == 0, c == DC - 1)
                ins.then_inc(score2_mm, 1)

            def turn_p2(s):
                wait(prob2_ok, "score2", 2)
                for k in range(DC):
                    for r in range(RT):
                        ins = e.transpose(halved(7)[:, k, r * P:r * P + P], hf[:, 0, r * D + k * P:r * D + k * P + P], ident[:, :])
                ins.then_inc(turn_p2_mm, 1)

            def z2(s):
                wait(turn_p2_ok, "turn_p2")
                for r in range(RT):
                    for k in range(DC):
                        ins = e.matmul(halved(5)[:, r, :], hf[:, 1, k * D + r * P:k * D + r * P + P], nx[:, s, k, :],
                                       start=k == 0, stop=k == DC - 1)
                ins.then_inc(z2_mm, 1)

            def turn_adj(s):
                for k in range(DC):
                    for r in range(RT):
                        ins = e.transpose(halved(7)[:, k, r * P:r * P + P], adjf[s][:, r, k * P:k * P + P], ident[:, :])
                ins.then_inc(adjT_mm, 1)

            def count(s, p):
                wait(mask_ok, "masks", 2)
                for l in range(2):
                    for k in range(DC):
                        ins = e.matmul(halved(5)[:, l, :], ones_r[:, :], mask[s][l][:, k, :], start=k == 0, stop=k == DC - 1)
                ins.then_inc(cnt_mm, 1)

            def agg(s, d):
                wait(hid_lo, "hidden")
                if d >= 2:
                    wait(agg_ok, "agg", 1, 2)
                for c in range(DC):
                    for k in range(DC):
                        for n, half in enumerate((hidh[s], hidl[s])):
                            ins = e.matmul(halved(6 + d % 2)[:, c, :], half[:, k, c * P:c * P + P], mask[s][d % 2][:, k, :],
                                           start=(k, n) == (0, 0), stop=(k, n) == (DC - 1, 1))
                ins.then_inc(agg_mm, 1)

            def wd(s, d):
                wait(agg_lo, "agg", 1, 0 if d == LABELS - 1 else 1)
                for c in range(DC):
                    for m in range(DC):
                        ins = mm3(halved(4)[:, m, :], w2("wd", DC * d + c, m * P, P),
                                  (hh[:, d % 2, c * D:c * D + D], hl[:, d % 2, c * D:c * D + D]),
                                  (d, c, m) == (0, 0, 0), (d, c) == (LABELS - 1, DC - 1), True)
                ins.then_inc(wd_mm, 1)

            def gates_hid(s):
                for b, name in ((5, "rh"), (6, "zh")):
                    for m in range(DC):
                        by_feature(b, name, m, first=m == 0, last=False, shared=True)
                for m in range(DC):
                    by_feature(7, "nh", m)

            def gates_out(s):
                wait(relu_lo, "relu")
                for b, name, fresh in ((5, "ri", False), (6, "zi", False), (4, "ni", True)):
                    for m in range(DC):
                        for c in range(DC):
                            ins = mm3(halved(b)[:, m, :], w2(name, c, m * P, P),
                                      (hh[:, 0, c * D:c * D + D], hl[:, 0, c * D:c * D + D]),
                                      fresh and c == 0, c == DC - 1, not fresh)
                ins.then_inc(out_mm, 1)

            def turn_back(s):
                wait(mix_ok, "gates", 4)
                for r in range(RT):
                    for c in range(DC):
                        ins = e.transpose(halved(5)[:, r, c * P:c * P + P], y[:, s, c, r * P:r * P + P], ident[:, :])
                ins.then_inc(back_mm, 1)

            walk(e, t, {"turn": turn, "qk": qk, "v": v, "score": score, "turn_p": turn_p, "pv": pv, "proj": proj,
                        "up": up, "down": down, "a2": a2, "score2": score2, "turn_p2": turn_p2, "z2": z2,
                        "turn_adj": turn_adj, "count": count, "agg": agg, "wd": wd, "gates_hid": gates_hid,
                        "gates_out": gates_out, "turn_back": turn_back})


def kernel(**inputs):
    import numpy as _np
    import concourse.bacc as _bacc
    from concourse import mybir as _mybir
    from concourse.bass_utils import run_bass_kernel_spmd as _run

    a = {k: _np.asarray(v) for k, v in inputs.items()}

    def chunks(w):
        return w.reshape(w.shape[0] // P, P, w.shape[1]).transpose(1, 0, 2).reshape(P, -1)

    mats = {"q0": a["L0_gnn_wq"], "k0": a["L0_gnn_wk"], "v0": a["L0_gnn_wv"], "o0": a["L0_gnn_wo"],
            "w1": a["L0_gnn_w1"], "w2": a["L0_gnn_w2"],
            "q1": a["L1_gnn_Wq"], "k1": a["L1_gnn_Wk"], "v1": a["L1_gnn_Wv"], "o1": a["L1_gnn_Wo"],
            "wd": a["L3_gnn_Wd"].T, "ri": a["L3_gnn_Wri"].T, "rh": a["L3_gnn_Wrh"].T, "zi": a["L3_gnn_Wzi"].T,
            "zh": a["L3_gnn_Wzh"].T, "ni": a["L3_gnn_Wni"].T, "nh": a["L3_gnn_Wnh"].T,
            "q2T": a["L2_gnn_Wq"].T, "k2T": a["L2_gnn_Wk"].T, "v2T": a["L2_gnn_Wv"].T, "o2": a["L2_gnn_Wo"]}
    vecs = {"ln1_g": a["L0_gnn_ln1_g"], "ln1_b": a["L0_gnn_ln1_b"], "ln2_g": a["L0_gnn_ln2_g"], "ln2_b": a["L0_gnn_ln2_b"],
            "bq0": a["L0_gnn_bq"], "bk0": a["L0_gnn_bk"], "bv0": a["L0_gnn_bv"],
            "bq1": a["L1_gnn_bq"], "bk1": a["L1_gnn_bk"], "bv1": a["L1_gnn_bv"],
            "bd": a["L3_gnn_bd"], "bri": a["L3_gnn_bri"], "brh": a["L3_gnn_brh"], "bzi": a["L3_gnn_bzi"],
            "bzh": a["L3_gnn_bzh"], "bni": a["L3_gnn_bni"], "bnh": a["L3_gnn_bnh"], "b1": a["L0_gnn_b1"]}
    rowv = {"bo0": a["L0_gnn_bo"], "b2": a["L0_gnn_b2"], "bo1": a["L1_gnn_bo"], "bo2": a["L2_gnn_bo"],
            "g1": a["L1_gnn_gamma"], "be1": a["L1_gnn_beta"], "g2": a["L2_gnn_gamma"], "be2": a["L2_gnn_beta"],
            "g3": a["L3_gnn_gamma"], "be3": a["L3_gnn_beta"]}
    arrays = {
        "x": _np.ascontiguousarray(a["x"]),
        "adj": _np.ascontiguousarray(a["adj"]),
        "weights": _np.concatenate([chunks(mats[n]) for g in GROUPS for n in g], axis=1),
        "cols": _np.ascontiguousarray(_np.concatenate([vecs[n].reshape(-1, P) for n in COLS]).T),
        "rows": _np.ascontiguousarray(_np.broadcast_to(_np.stack([rowv[n] for n in ROWV]), (P, len(ROWV), D))),
    }
    nc = _bacc.Bacc("TRN2", target_bir_lowering=False, num_devices=1)
    args = [nc.dram_tensor(n, v.shape, _mybir.dt.from_np(v.dtype), kind="ExternalInput").ap() for n, v in arrays.items()]
    args.append(nc.dram_tensor("out", a["x"].shape, _mybir.dt.float32, kind="ExternalOutput").ap())
    build(nc, *args)
    r = _run(nc, [arrays], core_ids=[0])
    return r.results[0]["out"]
```

```python
from contextlib import ExitStack

import numpy as np

import concourse.bass as bass
from concourse import mybir

F32 = mybir.dt.float32
F32R = mybir.dt.float32r
I32 = mybir.dt.int32
ALU = mybir.AluOpType
ACT = mybir.ActivationFunctionType

P = 128
D = 256
DC = D // P
RT = D // P
W = RT * D
H = 8
HD = D // H
HPC = P // HD
FF = 4 * D
UPS = FF // P // 2
LABELS = 4
SLOTS = 3
CW = 2
BIG = 1e38
QSCALE = float(1.0 / np.sqrt(HD))
LN_EPS = 1e-5
AGG_EPS = 1e-8

GROUPS = [["q0", "k0", "v0", "o0"], ["w1"], ["w2"], ["q1", "k1", "v1", "o1"],
          ["wd"], ["ri", "rh", "zi", "zh"], ["ni", "nh"], ["q2T", "k2T", "v2T", "o2"]]
WIDE = {"w1": 8, "w2": 8, "wd": 8}
NBLOCK = 0
WAT = {}
for _g in GROUPS[:-1]:
    for _n in _g:
        WAT[_n] = NBLOCK
        NBLOCK += WIDE.get(_n, DC)
WAT["qk2"], WAT["vo2"] = NBLOCK, NBLOCK + DC
NBLOCK += 2 * DC

SCALED = [0, 1, 3, 6, 7]
COLS = ["ln1_g", "ln1_b", "ln2_g", "ln2_b", "bq0", "bk0", "bv0", "bq1", "bk1", "bv1",
        "bd", "bri", "brh", "bzi", "bzh", "bni", "bnh", "b1"]
CAT = {n: DC * j for j, n in enumerate(COLS)}
NCOL = DC * (len(COLS) - 1) + FF // P
ROWV = ["bo0", "b2", "bo1", "bo2", "g1", "be1", "g2", "be2", "g3", "be3"]
RAT = {n: j for j, n in enumerate(ROWV)}
BAT = {"q0": 0, "k0": 2, "v0": 4, "q1": 6, "r": 8, "z": 10, "nh": 12, "b1": 14}



def attention(s, a):
    steps = []
    for t in range(H + 3):
        if t < H:
            steps.append(("score", s, a, t))
        if 2 <= t <= H + 1:
            steps.append(("turn_p", s, a, t - 2))
        if t >= 3:
            steps.append(("pv", s, a, t - 3))
    return steps + [("heads", s, a)]


def before(s):
    return [("stats", s, "in"), "*", "*", ("norm", s, "in"), ("prep", s), ("residual", s, "in"), "*",
            ("turn", s, "in"), "*", "*", ("qk", s, 0), ("v", s, 0)]


def middle(s):
    out = [("turn", s, "heads"), "*", "back", "*", "centre", ("proj", s, "o0"), "norm", "*", ("residual", s, "mid"),
           ("stats", s, "mid")]
    out += ["*"] * 3 + [("norm", s, "mid")] + ["*"] * 4 + [("turn", s, "norm")] + ["*"] * 7
    for j in range(UPS + 2):
        if j < UPS:
            out.append(("up", s, j))
        if j >= 2:
            out.append(("down", s, j - 2))
    return out + [("mlp_sum", s), ("keeps", s)] + ["*"] * 2 + [("turn", s, "sum"), ("residual", s, "x2")] + ["*"] * 6 + [
        ("qk", s, 1), ("v", s, 1)]


def late(s, nxt):
    out = [("turn_adj", s), ("turn", s, "heads"), "*", "back", "*", "centre", ("proj", s, "o1"), "norm", "*",
           ("stats", s, "l1"), ("centre", s, "l1")]
    out += ["*"] * 3 + [("norm", s, "l1"), ("residual", s, "l1"), "*"]
    out += [("turn", s, "norm")] + ["*"] * 2 + [("a2", s), ("masks", s)] + ["*"] * 2 + [("score2", s)]
    if nxt:
        out += [("load_adj", s, 1), ("prep", s)]
    out += [("count", s)] + ["*"] * 3 + [("turn_p2", s)] + ["*"] + [("z2", s), "*", ("turn", s, "z2"), "*", "*"]
    out += [("proj", s, "vo2"), ("spread", s, 0), ("spread", s, 1)]
    if nxt:
        out += [("load_x", s, 1)]
    out += [("stats", s, "l2"), ("centre", s, "l2")] + ["*"] * 3
    out += [("norm", s, "l2"), ("hidden", s), "*", ("turn", s, "norm"), "*"] + [("agg", s, 0), ("agg", s, 1), ("agg_low", s, 0)]
    out += [("gates_hid", s, "r"), ("wd", s, 0), ("agg", s, 2), ("agg_low", s, 1)]
    if nxt:
        out += [("stats", s, "in")]
    out += [("wd", s, 1), ("agg", s, 3), ("agg_low", s, 2), ("wd", s, 2), ("agg_low", s, 3)]
    if nxt:
        out += [("norm", s, "in")]
    out += [("wd", s, 3), ("relu", s), ("gates_hid", s, "zn")]
    if nxt:
        out += [("turn", s, "in")]
    out += [("gates_out", s), ("gates", s)]
    if nxt:
        out += ["*", "*", ("qk", s, 0), ("v", s, 0), ("residual", s, "in")]
    return out


def after(s, lin):
    last = {"back": [("turn_back", s)], "centre": [("stats", s, "fin"), ("centre", s, "fin")],
            "norm": [("norm", s, "fin"), ("store", s)]}
    return [step for one in lin for step in (last[one] if one in last else [one])]


def first(lin):
    return [step for step in lin if step not in ("back", "centre", "norm")]


def slot(att, lin):
    att, out = list(att), []
    for step in lin:
        if step != "*":
            out.append(step)
        elif att:
            out.append(att.pop(0))
    return out + att


PROLOGUE = ([("load_adj", 0, 0), ("load_x", 0, 0), ("load_adj", 1, 0), ("load_x", 1, 0)] + slot([], before(0))
            + slot(attention(0, 0), before(1)) + slot(attention(1, 0), first(middle(0)))
            + slot(attention(0, 1), first(middle(1))))
BODY = (slot(attention(1, 1), first(late(0, True))) + slot(attention(0, 0), after(0, late(1, True)))
        + slot(attention(1, 0), after(1, middle(0))) + slot(attention(0, 1), first(middle(1))))
EPILOGUE = (slot(attention(1, 1), first(late(0, False))) + slot([], after(0, late(1, False)))
            + after(1, ["back", "centre", "norm"]))


class Tally:

    def __init__(self, loops):
        self.loops, self.i, self.base, self.rate, self.here = loops, None, {}, {}, {}
        for step in BODY:
            self.rate[step[0]] = self.rate.get(step[0], 0) + 1
            self.rate[step[:2]] = self.rate.get(step[:2], 0) + 1

    def enter(self, step):
        for key in (step[0], step[:2]):
            self.here[key] = self.here.get(key, 0) + 1

    def loop_begins(self, i):
        self.base, self.here, self.i = self.here, {}, i

    def loop_ends(self):
        self.i = None
        keys = set(self.rate) | set(self.base)
        self.here = {k: self.base.get(k, 0) + self.loops * self.rate.get(k, 0) for k in keys}
        self.base = {}

    def value(self, key, per, less):
        n = per * (self.base.get(key, 0) + self.here.get(key, 0)) - less
        if self.i is None or not self.rate.get(key):
            return n
        return self.i * (per * self.rate[key]) + n


def build(nc, x, adj, weights, cols, rows, out):
    loops = x.shape[0] // 2 - 1
    x_v = x.rearrange("b (q p) d -> b p q d", p=P)
    adj_v = adj.rearrange("b (q p) k -> b p q k", p=P)
    out_v = out.rearrange("b (q p) d -> b p q d", p=P)

    with ExitStack() as ctx:
        def sb(name, shape, dt=F32):
            return ctx.enter_context(nc.sbuf_tensor(name, shape, dt))

        def sem(name):
            return ctx.enter_context(nc.semaphore(name))

        WH = sb("WH", [P, NBLOCK, D], F32R)
        WL = sb("WL", [P, NBLOCK, D], F32R)
        colv = sb("colv", [P, NCOL])
        rowv = sb("rowv", [P, len(ROWV), D])
        bias = sb("bias", [P, 14 + FF // P])
        halves = sb("halves", [P, 2 * DC])
        power = sb("power", [P, RT])
        spare = sb("spare", [P, 1])
        ident = sb("ident", [P, P])
        ones = sb("ones", [P, P])
        ones_r = sb("ones_r", [P, CW], F32R)
        xin = sb("xin", [P, 2, RT, D])
        adjb = sb("adjb", [P, 2, RT, D], I32)
        nb = sb("nb", [P, 2, 2, W])
        res = sb("res", [P, 2, RT, D])
        y = sb("y", [P, 2, RT, D])
        nx = sb("nx", [P, 2, RT, D])
        qh = sb("qh", [P, 2, DC, D], F32R)
        ql = sb("ql", [P, 2, DC, D], F32R)
        kh = sb("kh", [P, 2, DC, D], F32R)
        kl = sb("kl", [P, 2, DC, D], F32R)
        V = sb("V", [P, 2, RT, D])
        keep = sb("keep", [P, 2, RT])
        tTh = sb("tTh", [P, 2, DC, D], F32R)
        tTl = sb("tTl", [P, 2, DC, D], F32R)
        hf = sb("hf", [P, 2, W])
        hh = sb("hh", [P, 2, W], F32R)
        hl = sb("hl", [P, 2, W], F32R)
        rc = sb("rc", [P, LABELS, D])
        rcnt = sb("rcnt", [P, LABELS * RT])
        st = sb("st", [P, RT, 6])
        mv = sb("mv", [P, RT, 2])
        rstd = sb("rstd", [P, 2, RT])
        nmax2 = sb("nmax2", [P, RT])
        rsum2 = sb("rsum2", [P, RT])
        rec2 = sb("rec2", [P, RT])
        S = sb("S", [P, SLOTS, RT, D])
        PT = sb("PT", [P, 2, DC, D])
        nmax = sb("nmax", [P, SLOTS, RT])
        rsum = sb("rsum", [P, RT, H])
        rec = sb("rec", [P, RT, H])
        bank = ctx.enter_context(nc.psum_tensor("bank", [P, 8, W], F32))

        def halved(b):
            return bank[:, b, :].rearrange("p (c n) -> p c n", c=2)

        def flat(ap):
            return ap.rearrange("p a b -> p (a b)")

        def f32(ap):
            return ap.bitcast(F32)

        stage = nb[:, :, :, :].rearrange("p a b c -> p (a b c)")
        nbias = [[nb[:, s, a, :].rearrange("p (r k) -> p r k", r=RT) for a in range(2)] for s in range(2)]
        adjf = [f32(adjb[:, s, :, :]) for s in range(2)]
        adjT = [nbias[s][0] for s in range(2)]
        mask = [[qh[:, s, :, :], ql[:, s, :, :], tTh[:, 1, :, :], tTl[:, 1, :, :]] for s in range(2)]
        rspread = [[buf[:, s, :, :].rearrange("p r (n m) -> p (r n) m", m=P) for buf in (V, xin)] for s in range(2)]
        vb = S[:, 0, :, 0:P]
        hidh = [kh[:, s, :, :] for s in range(2)]
        hidl = [kl[:, s, :, :] for s in range(2)]

        def wt(half, name, c, lo, hi):
            n = FF // D if name == "w1" else 1
            a = WAT[name] + c * n
            return half[:, a:a + n, :].rearrange("p b d -> p (b d)")[:, lo:hi]

        def col(name, c=0):
            return colv[:, CAT[name] + c:CAT[name] + c + 1]

        def bcol(name, c=0):
            return bias[:, BAT[name] + c:BAT[name] + c + 1]

        def row(name):
            return rowv[:, RAT[name], :]

        s_ident0, s_ident, s_const = sem("s_ident0"), sem("s_ident"), sem("s_const")
        waited = sem("waited")
        s_vecs, s_staged = sem("s_vecs"), sem("s_staged")
        s_fold, s_bias, s_scaled = sem("s_fold"), sem("s_bias"), sem("s_scaled")
        s_whi, s_wlo, s_prod, s_vb, s_rowfix = sem("s_whi"), sem("s_wlo"), sem("s_prod"), sem("s_vb"), sem("s_rowfix")
        x_in = [sem("x_in0"), sem("x_in1")]
        adj_in = [sem("adj_in0"), sem("adj_in1")]
        stored = [sem("stored0"), sem("stored1")]
        mask_bias = sem("mask_bias")
        prep_step = sem("prep_step")
        keep_ok = sem("keep_ok")
        stat_ok = sem("stat_ok")
        mean_ok = sem("mean_ok")
        var_ok = sem("var_ok")
        rstd_ok = sem("rstd_ok")
        cent_ok = sem("cent_ok")
        norm_ok = sem("norm_ok")
        res_ok = sem("res_ok")
        turn_mm = sem("turn_mm")
        turn_hi, turn_lo = sem("turn_hi"), sem("turn_lo")
        qk_mm = sem("qk_mm")
        qk_hi, qk_lo = sem("qk_hi"), sem("qk_lo")
        v_mm, v_ok = sem("v_mm"), sem("v_ok")
        score_mm = sem("score_mm")
        score_max = sem("score_max")
        prob_ok = sem("prob_ok")
        turn_p_mm, turn_p_ok = sem("turn_p_mm"), sem("turn_p_ok")
        pv_mm = sem("pv_mm")
        rec_ok, heads_ok = sem("rec_ok"), sem("heads_ok")
        proj_mm, proj_ok = sem("proj_mm"), sem("proj_ok")
        up_mm = sem("up_mm")
        up_act = sem("up_act")
        up_hi, up_lo = sem("up_hi"), sem("up_lo")
        down_mm, sum_ok = sem("down_mm"), sem("sum_ok")
        a2_mm, a2_hi, a2_lo = sem("a2_mm"), sem("a2_hi"), sem("a2_lo")
        score2_mm = sem("score2_mm")
        score2_max, prob2_ok = sem("score2_max"), sem("prob2_ok")
        turn_p2_mm, turn_p2_ok = sem("turn_p2_mm"), sem("turn_p2_ok")
        z2_mm, rec2_ok, z2_ok = sem("z2_mm"), sem("rec2_ok"), sem("z2_ok")
        hid_hi, hid_lo = sem("hid_hi"), sem("hid_lo")
        adjT_mm, adjT_ok = sem("adjT_mm"), sem("adjT_ok")
        mask_ok = sem("mask_ok")
        table_in = sem("table_in")
        cnt_mm, cnt_eps, rc_ok, rcol_ok = sem("cnt_mm"), sem("cnt_eps"), sem("rc_ok"), sem("rcol_ok")
        spread_mm, spread_ok = sem("spread_mm"), sem("spread_ok")
        agg_mm, agg_ok, agg_hi, agg_lo = sem("agg_mm"), sem("agg_ok"), sem("agg_hi"), sem("agg_lo")
        wd_mm = sem("wd_mm")
        relu_ok = sem("relu_ok")
        relu_hi, relu_lo = sem("relu_hi"), sem("relu_lo")
        hid_mm, out_mm = sem("hid_mm"), sem("out_mm")
        gate_act = sem("gate_act")
        pre_ok = sem("pre_ok")
        cand_ok = sem("cand_ok")
        mix_ok = sem("mix_ok")
        back_mm = sem("back_mm")

        block = ctx.enter_context(nc.Block())

        def walk(e, tally, ops):
            def run(steps):
                for step in steps:
                    tally.enter(step)
                    if step[0] in ops:
                        ops[step[0]](*step[1:])

            run(PROLOGUE)
            with e.Fori(0, loops) as i:
                tally.loop_begins(i)
                run(BODY)
            tally.loop_ends()
            run(EPILOGUE)

        def waiter(e, tally):
            def wait(s, key, per=1, less=0, alone=False):
                ins = e.wait_ge(s, tally.value(key, per, less))
                if alone:
                    ins.then_inc(waited, 1)
            return wait

        def group_span(j):
            return WAT[GROUPS[j][0]], sum(WIDE.get(n, DC) for n in GROUPS[j])

        @block.sync
        def _(e):
            t = Tally(loops)
            wait = waiter(e, t)
            e.dma_start(colv[:, :], cols).then_inc(s_vecs, 16)
            e.dma_start(rowv[:, :, :], rows).then_inc(s_vecs, 16)
            at = 0
            for j, names in enumerate(GROUPS):
                n = sum(WIDE.get(m, DC) for m in names) * D
                if j >= 1:
                    e.wait_ge(s_wlo, j)
                e.dma_start(stage[:, 0:n], weights[:, at:at + n]).then_inc(s_staged, 16)
                at += n

            def load_adj(s, ahead):
                g = s if t.i is None else t.i * 2 + (2 * ahead + s)
                if ahead:
                    wait(adjT_mm, "turn_adj", alone=True)
                e.dma_start(adjb[:, s, :, :], adj_v[bass.ds(g, 1), :, :, :].rearrange("a p r d -> (a p) r d")).then_inc(adj_in[s], 16)

            def load_x(s, ahead):
                g = s if t.i is None else t.i * 2 + (2 * ahead + s)
                if ahead:
                    wait(turn_hi, "turn", alone=True)
                    wait(res_ok, "residual", alone=True)
                    wait(spread_mm, "spread", alone=True)
                e.dma_start(xin[:, s, :, :], x_v[bass.ds(g, 1), :, :, :].rearrange("a p r d -> (a p) r d")).then_inc(x_in[s], 16)

            def store(s):
                g = 2 * loops + s if t.i is None else t.i * 2 + s
                wait(norm_ok, "norm", 2, alone=True)
                e.dma_start(out_v[bass.ds(g, 1), :, :, :].rearrange("a p r d -> (a p) r d"), y[:, s, :, :]).then_inc(stored[s], 16)

            walk(e, t, {"load_adj": load_adj, "load_x": load_x, "store": store})
            for s in range(2):
                wait(stored[s], ("store", s), 16)

        @block.gpsimd
        def _(e):
            t = Tally(loops)
            wait = waiter(e, t)
            e.memset(ident[:, :], 0.0).then_inc(s_ident0, 1)
            e.memset(power[:, :], -0.5).then_inc(s_const, 1)
            e.memset(ones[:, :], 1.0).then_inc(s_const, 1)
            e.wait_ge(s_ident0, 1)
            e.affine_select(out=ident[:, :], in_=ident[:, :], compare_op=ALU.not_equal, fill=1.0,
                            base=0, pattern=[[-1, P]], channel_multiplier=1).then_inc(s_ident, 1)
            e.wait_ge(s_const, 2)
            e.wait_ge(s_rowfix, 2)

            def stats(s, which):
                wait(var_ok, "stats")
                e.tensor_tensor(rstd[:, s, :], rstd[:, s, :], power[:, :], ALU.pow).then_inc(rstd_ok, 1)

            def prep(s):
                f, n0, n1 = flat(adjf[s]), nb[:, s, 0, :], nb[:, s, 1, :]
                if t.i is not None:
                    wait(mask_ok, "masks", LABELS)
                    wait(score2_max, "score2", 2)
                wait(adj_in[s], ("load_adj", s), 16, alone=True)
                e.tensor_copy(f, flat(adjb[:, s, :, :])).then_inc(mask_bias, 1)
                wait(mask_bias, "prep", 4, 3, alone=True)
                e.tensor_scalar(n0, f, -0.1, 1.0, ALU.mult, ALU.mult).then_inc(prep_step, 1)
                e.tensor_scalar(n1, f, 0.0, BIG, ALU.is_le, ALU.mult).then_inc(prep_step, 1)
                wait(prep_step, "prep", 3, 1)
                e.tensor_tensor(n0, n0, f, ALU.mult).then_inc(prep_step, 1)
                wait(prep_step, "prep", 3)
                e.tensor_tensor(n0, n0, n1, ALU.add).then_inc(mask_bias, 1)
                wait(mask_bias, "prep", 4, 2, alone=True)
                e.tensor_scalar(n1, f, 0.0, BIG, ALU.is_equal, ALU.mult).then_inc(mask_bias, 2)

            def residual(s, which):
                src, name = {"in": (xin, "bo0"), "mid": (y, "b2"), "x2": (y, "bo1"), "l1": (nx, "bo2")}[which]
                if which == "in":
                    wait(x_in[s], ("load_x", s), 16)
                    if t.i is not None:
                        wait(mix_ok, "gates", 4)
                elif which == "mid":
                    wait(proj_ok, "proj")
                elif which == "x2":
                    wait(sum_ok, "mlp_sum")
                else:
                    wait(norm_ok, "norm", 2)
                for r in range(RT):
                    op = e.tensor_tensor(res[:, s, r, :], src[:, s, r, :], row(name), ALU.add)
                op.then_inc(res_ok, 1)

            def high(slot, done):
                e.tensor_scalar(hh[:, slot, :], hf[:, slot, :], 1.0, 0.0, ALU.mult, ALU.add).then_inc(done, 1)

            def up(s, j):
                if j >= 2:
                    wait(down_mm, "down", 1, -1)
                wait(up_act, "up", 2, alone=True)
                high(j % 2, up_hi)

            def hidden(s):
                wait(norm_ok, "norm", 2, alone=True)
                e.tensor_scalar(flat(hidh[s]), flat(nx[:, s, :, :]), 1.0, 0.0, ALU.mult, ALU.add).then_inc(hid_hi, 1)

            def agg(s, d):
                if d >= 2:
                    wait(wd_mm, "wd")
                wait(agg_ok, "agg", alone=True)
                high(d % 2, agg_hi)

            def relu(s):
                wait(relu_ok, "relu", 2, alone=True)
                high(0, relu_hi)

            walk(e, t, {"prep": prep, "stats": stats, "residual": residual, "up": up, "hidden": hidden, "agg": agg,
                        "relu": relu})

        @block.scalar
        def _(e):
            t = Tally(loops)
            wait = waiter(e, t)
            for j in range(len(GROUPS) - 1):
                a, n = group_span(j)
                e.wait_ge(s_staged, 16 * (j + 1))
                if j in SCALED:
                    e.wait_ge(s_scaled, SCALED.index(j) + 1)
                e.activation(flat(WH[:, a:a + n, :]), stage[:, 0:n * D], ACT.Copy).then_inc(s_whi, 1)
            for j, name in enumerate(("qk2", "vo2")):
                e.wait_ge(s_prod, j + 1)
                e.activation(flat(WH[:, WAT[name]:WAT[name] + DC, :]), bank[:, 4 + j, :], ACT.Copy).then_inc(s_whi, 1)

            def copy(dst, src, done):
                e.activation(dst, src, ACT.Copy).then_inc(done, 1)

            def turn(s, src):
                wait(turn_mm, "turn")
                copy(flat(tTh[:, int(src == "in"), :, :]), bank[:, 4, :], turn_hi)

            def qk(s, a):
                for n, (dst, b) in enumerate(((qh, 5), (kh, 6))):
                    wait(qk_mm, "qk", 2, 1 - n)
                    for m in range(DC):
                        bc = bcol("q%d" % a, m) if n == 0 else (bcol("k0", m) if a == 0 else col("bk1", m))
                        e.activation(dst[:, s, m, :], halved(b)[:, m, :], ACT.Identity, bias=bc).then_inc(qk_hi, 1)

            def v(s, a):
                wait(v_mm, "v")
                copy(flat(V[:, s, :, :]), bank[:, 7, :], v_ok)

            def score(s, a, h):
                for r in range(RT):
                    wait(score_max, "score", 2, 1 - r)
                    e.activation(S[:, h % SLOTS, r, :], S[:, h % SLOTS, r, :], ACT.Exp, bias=nmax[:, h % SLOTS, r:r + 1],
                                 scale=-1.0, accum_out=rsum[:, r, h:h + 1]).then_inc(prob_ok, 1)

            def turn_p(s, a, h):
                wait(turn_p_mm, "turn_p")
                if h >= 2:
                    wait(pv_mm, "pv")
                copy(flat(PT[:, h % 2, :, :]), bank[:, 2, :], turn_p_ok)

            def up(s, j):
                wait(up_mm, "up")
                if j >= 2:
                    wait(up_lo, "up", 1, 2)
                for f in range(2):
                    e.activation(hf[:, j % 2, f * D:f * D + D], halved(6 + j % 2)[:, f, :], ACT.Gelu,
                                 bias=bcol("b1", 2 * j + f)).then_inc(up_act, 1)

            def mlp_sum(s):
                e.activation(spare[:, :], power[:, 0:1], ACT.Exp).then_inc(table_in, 1)

            def a2(s):
                wait(a2_mm, "a2")
                copy(flat(kh[:, s, :, :]), bank[:, 5, :], a2_hi)

            def score2(s):
                for r in range(RT):
                    wait(score2_max, "score2", 2, 1 - r)
                    e.activation(hf[:, 0, r * D:r * D + D], hf[:, 0, r * D:r * D + D], ACT.Exp, bias=nmax2[:, r:r + 1],
                                 scale=-1.0, accum_out=rsum2[:, r:r + 1]).then_inc(prob2_ok, 1)

            def turn_p2(s):
                wait(turn_p2_mm, "turn_p2")
                copy(hf[:, 1, :], bank[:, 7, :], turn_p2_ok)

            def turn_adj(s):
                wait(adjT_mm, "turn_adj")
                copy(flat(adjT[s]), bank[:, 7, :], adjT_ok)

            def spread(s, p):
                wait(spread_mm, "spread")
                copy(flat(rc[:, 2 * p:2 * p + 2, :]), bank[:, 6 + p, :], spread_ok)

            def relu(s):
                wait(wd_mm, "wd")
                for m in range(DC):
                    e.activation(hf[:, 0, m * D:m * D + D], halved(4)[:, m, :], ACT.Relu, bias=col("bd", m)).then_inc(relu_ok, 1)

            def gates(s):
                wait(hid_mm, "gates_out")
                for m in range(DC):
                    e.activation(res[:, s, m, :], halved(7)[:, m, :], ACT.Identity, bias=bcol("nh", m)).then_inc(gate_act, 1)
                for less, b, name, dst in ((2, 5, "r", hf[:, 1, :]), (1, 6, "z", hf[:, 0, :])):
                    wait(out_mm, "gates_out", 3, less)
                    for m in range(DC):
                        e.activation(dst[:, m * D:m * D + D], halved(b)[:, m, :], ACT.Tanh, bias=bcol(name, m),
                                     scale=0.5).then_inc(gate_act, 1)
                wait(pre_ok, "gates", 2)
                for m in range(DC):
                    e.activation(res[:, s, m, :], hf[:, 1, m * D:m * D + D], ACT.Tanh, bias=col("bni", m)).then_inc(cand_ok, 1)

            walk(e, t, {"turn": turn, "qk": qk, "v": v, "score": score, "turn_p": turn_p, "up": up, "mlp_sum": mlp_sum, "a2": a2,
                        "score2": score2, "turn_p2": turn_p2, "turn_adj": turn_adj, "spread": spread, "relu": relu,
                        "gates": gates})

        @block.vector
        def _(e):
            t = Tally(loops)
            wait = waiter(e, t)
            tsc, tt, stt = e.tensor_scalar, e.tensor_tensor, e.scalar_tensor_tensor
            e.wait_ge(s_vecs, 32)
            e.wait_ge(s_const, 2)
            tt(halves[:, 0:DC], colv[:, CAT["bri"]:CAT["bri"] + DC], colv[:, CAT["brh"]:CAT["brh"] + DC], ALU.add).then_inc(s_bias, 1)
            tt(halves[:, DC:2 * DC], colv[:, CAT["bzi"]:CAT["bzi"] + DC], colv[:, CAT["bzh"]:CAT["bzh"] + DC], ALU.add).then_inc(s_bias, 1)
            e.wait_ge(s_bias, 2)
            tsc(bias[:, BAT["r"]:BAT["r"] + 2 * DC], halves[:, :], 0.5, None, ALU.mult).then_inc(s_bias, 1)
            tsc(bias[:, BAT["nh"]:BAT["nh"] + DC], colv[:, CAT["bnh"]:CAT["bnh"] + DC], 0.5, None, ALU.mult).then_inc(s_bias, 1)
            tsc(bias[:, BAT["q1"]:BAT["q1"] + DC], colv[:, CAT["bq1"]:CAT["bq1"] + DC], -QSCALE, None, ALU.mult).then_inc(s_bias, 1)
            tsc(ones_r[:, :], ones[:, 0:CW], 1.0, None, ALU.mult).then_inc(s_bias, 1)

            def spread(src, n):
                for c in range(DC):
                    tsc(vb[:, c, :], ones[:, :], src(c), None, ALU.mult).then_inc(s_vb, 1)

            def scale(lo, n, by, const):
                part = stage[:, lo:lo + n]
                if by is None:
                    return tsc(part, part, const, None, ALU.mult)
                return tsc(part, part, by, const, ALU.mult, ALU.mult)

            def split_low(j, a, n, src):
                e.wait_ge(s_whi, j + 1)
                tt(flat(WL[:, a:a + n, :]), src, f32(flat(WH[:, a:a + n, :])), ALU.subtract).then_inc(s_wlo, 1)

            for j in range(len(GROUPS)):
                e.wait_ge(s_staged, 16 * (j + 1))
                if j == 0:
                    e.wait_ge(s_fold, 1)
                    for n, name in enumerate(("q0", "k0", "v0")):
                        tt(bias[:, BAT[name]:BAT[name] + DC], bank[:, 4, DC * n:DC * n + DC],
                           colv[:, CAT["b" + name]:CAT["b" + name] + DC], ALU.add).then_inc(s_bias, 1)
                    e.wait_ge(s_bias, 9)
                    tsc(bias[:, BAT["q0"]:BAT["q0"] + DC], bias[:, BAT["q0"]:BAT["q0"] + DC], -QSCALE, None, ALU.mult).then_inc(s_bias, 1)
                    spread(lambda c: bcol("v0", c), 0)
                    e.wait_ge(s_fold, 2)
                    tt(row("bo0"), bank[:, 5, 0:D], row("bo0"), ALU.add).then_inc(s_rowfix, 1)
                    for w, const in enumerate((-QSCALE, 1.0, 1.0)):
                        for c in range(DC):
                            ins = scale((DC * w + c) * D, D, col("ln1_g", c), const)
                    ins.then_inc(s_scaled, 1)
                elif j == 1:
                    e.wait_ge(s_fold, 3)
                    tt(bias[:, BAT["b1"]:BAT["b1"] + FF // P], bank[:, 6, 0:FF // P],
                       colv[:, CAT["b1"]:CAT["b1"] + FF // P], ALU.add).then_inc(s_bias, 1)
                    for c in range(DC):
                        ins = scale(c * FF, FF, col("ln2_g", c), 1.0)
                    ins.then_inc(s_scaled, 1)
                elif j == 3:
                    spread(lambda c: col("bv1", c), 1)
                    e.wait_ge(s_fold, 4)
                    tt(row("bo1"), bank[:, 7, 0:D], row("bo1"), ALU.add).then_inc(s_rowfix, 1)
                    scale(0, DC * D, None, -QSCALE).then_inc(s_scaled, 1)
                elif j == 6:
                    scale(DC * D, DC * D, None, 0.5).then_inc(s_scaled, 1)
                elif j == 7:
                    scale(0, DC * D, None, -1.0 / float(np.sqrt(D))).then_inc(s_scaled, 1)
                if j < len(GROUPS) - 1:
                    a, n = group_span(j)
                    split_low(j, a, n, stage[:, 0:n * D])
            for n, name in enumerate(("qk2", "vo2")):
                split_low(len(GROUPS) - 1 + n, WAT[name], DC, bank[:, 4 + n, :])

            def source(s, which):
                return halved(6) if which == "fin" else (xin if which == "in" else y)[:, s, :, :]

            def keeps(s):
                wait(mask_bias, "prep", 4)
                e.tensor_reduce(keep[:, s, :], nbias[s][1], mybir.AxisListType.X, ALU.min).then_inc(keep_ok, 1)
                wait(keep_ok, "keeps", 2, 1)
                tsc(keep[:, s, :], keep[:, s, :], 1.0, None, ALU.is_lt).then_inc(keep_ok, 1)

            def stats(s, which):
                src = source(s, which)
                if which == "in":
                    wait(x_in[s], ("load_x", s), 16)
                elif which == "fin":
                    wait(back_mm, "turn_back")
                else:
                    wait(proj_ok, "proj")
                for r in range(RT):
                    e.bn_stats(st[:, r, :], src[:, r, :]).then_inc(stat_ok, 1)
                for r in range(RT):
                    wait(stat_ok, "stats", 2, 1 - r, alone=True)
                    e.bn_aggr(mv[:, r, :], st[:, r, :]).then_inc(mean_ok, 1)
                wait(mean_ok, "stats", 2)
                tsc(rstd[:, s, :], mv[:, :, 1], LN_EPS, None, ALU.add).then_inc(var_ok, 1)

            def gains(which):
                n = {"l1": "1", "l2": "2", "fin": "3"}[which]
                return row("g" + n), row("be" + n)

            def centre(s, which):
                src, dst = source(s, which), (y if which == "fin" else nx)
                for r in range(RT):
                    wait(mean_ok, "stats", 2, 1 - r)
                    stt(dst[:, s, r, :], src[:, r, :], mv[:, r, 0:1], gains(which)[0], ALU.subtract, ALU.mult).then_inc(cent_ok, 1)

            def norm(s, which):
                wait(rstd_ok, "stats")
                for r in range(RT):
                    if which in ("in", "mid"):
                        tsc(nx[:, s, r, :], source(s, which)[:, r, :], mv[:, r, 0:1], rstd[:, s, r:r + 1],
                            ALU.subtract, ALU.mult).then_inc(norm_ok, 1)
                    else:
                        dst = (y if which == "fin" else nx)[:, s, r, :]
                        wait(cent_ok, "centre", 2, 1 - r)
                        stt(dst, dst, rstd[:, s, r:r + 1], gains(which)[1], ALU.mult, ALU.add).then_inc(norm_ok, 1)

            def turn(s, src):
                wait(turn_hi, "turn")
                w = int(src == "in")
                tt(flat(tTl[:, w, :, :]), bank[:, 4, :], f32(flat(tTh[:, w, :, :])), ALU.subtract).then_inc(turn_lo, 1)

            def qk(s, a):
                for n, (hi, lo, b) in enumerate(((qh, ql, 5), (kh, kl, 6))):
                    wait(qk_hi, "qk", 4, 2 - 2 * n)
                    for m in range(DC):
                        bc = bcol("q%d" % a, m) if n == 0 else (bcol("k0", m) if a == 0 else col("bk1", m))
                        stt(lo[:, s, m, :], halved(b)[:, m, :], bc, f32(hi[:, s, m, :]), ALU.add, ALU.subtract).then_inc(qk_lo, 1)

            def score(s, a, h):
                if h >= SLOTS:
                    wait(turn_p_mm, "turn_p")
                if h == 0:
                    wait(mask_bias, "prep", 4)
                wait(score_mm, "score", alone=True)
                for r in range(RT):
                    e.tensor_tensor_reduce(S[:, h % SLOTS, r, :], halved(h % 2)[:, r, :], nbias[s][a][:, r, :], 1.0, 3.3e38,
                                           ALU.add, ALU.min, nmax[:, h % SLOTS, r:r + 1]).then_inc(score_max, 1)

            def heads(s, a):
                wait(pv_mm, "pv")
                e.reciprocal(flat(rec[:, :, :]), flat(rsum[:, :, :])).then_inc(rec_ok, 1)
                wait(rec_ok, "heads")
                tt(flat(nx[:, s, :, :]).rearrange("p (n e) -> p n e", e=HD),
                   bank[:, 3, :].rearrange("p (n e) -> p n e", e=HD),
                   flat(rec[:, :, :]).unsqueeze(2).to_broadcast([P, RT * H, HD]), ALU.mult).then_inc(heads_ok, 1)

            def proj(s, name):
                if name == "o0" and t.i is not None:
                    wait(stored[s], ("store", s), 16)
                wait(proj_mm, "proj")
                wait(res_ok, "residual")
                tt(flat(y[:, s, :, :]), bank[:, 5, :], flat(res[:, s, :, :]), ALU.add).then_inc(proj_ok, 1)

            def low(slot, done):
                tt(hl[:, slot, :], hf[:, slot, :], f32(hh[:, slot, :]), ALU.subtract).then_inc(done, 1)

            def up(s, j):
                wait(up_hi, "up")
                low(j % 2, up_lo)

            def agg_low(s, d):
                wait(agg_hi, "agg", 1, 0 if d == LABELS - 1 else 1)
                low(d % 2, agg_lo)

            def mlp_sum(s):
                wait(down_mm, "down")
                wait(res_ok, "residual")
                tt(flat(y[:, s, :, :]), bank[:, 5, :], flat(res[:, s, :, :]), ALU.add).then_inc(sum_ok, 1)

            def a2(s):
                wait(a2_hi, "a2")
                tt(flat(kl[:, s, :, :]), bank[:, 5, :], f32(flat(kh[:, s, :, :])), ALU.subtract).then_inc(a2_lo, 1)

            def score2(s):
                wait(score2_mm, "score2", alone=True)
                for r in range(RT):
                    e.tensor_tensor_reduce(hf[:, 0, r * D:r * D + D], halved(6)[:, r, :], nbias[s][1][:, r, :],
                                           keep[:, s, r:r + 1], 3.3e38, ALU.add, ALU.min, nmax2[:, r:r + 1]).then_inc(score2_max, 1)

            def z2(s):
                wait(z2_mm, "z2")
                e.reciprocal(rec2[:, :], rsum2[:, :]).then_inc(rec2_ok, 1)
                wait(rec2_ok, "z2")
                for r in range(RT):
                    tsc(y[:, s, r, :], halved(5)[:, r, :], rec2[:, r:r + 1], None, ALU.mult).then_inc(z2_ok, 1)

            def hidden(s):
                wait(hid_hi, "hidden")
                tt(flat(hidl[s]), flat(nx[:, s, :, :]), f32(flat(hidh[s])), ALU.subtract).then_inc(hid_lo, 1)

            def masks(s):
                wait(adjT_ok, "turn_adj")
                for l in range(LABELS):
                    tsc(flat(mask[s][l]), flat(adjT[s]), float(l + 1), None, ALU.is_equal).then_inc(mask_ok, 1)

            def count(s):
                wait(cnt_mm, "count")
                tsc(rcnt[:, :], bank[:, 4, 0:LABELS * RT * CW:CW], AGG_EPS, None, ALU.add).then_inc(cnt_eps, 1)
                wait(cnt_eps, "count")
                e.reciprocal(rcnt[:, :], rcnt[:, :]).then_inc(rc_ok, 1)
                wait(rc_ok, "count")
                for n in range(LABELS * RT):
                    ins = tsc(rspread[s][n // 4][:, n % 4, :], ones[:, :], rcnt[:, n:n + 1], None, ALU.mult)
                ins.then_inc(rcol_ok, 1)

            def agg(s, d):
                wait(agg_mm, "agg")
                wait(spread_ok, "spread")
                if d >= 2:
                    wait(agg_lo, "agg_low")
                tt(hf[:, d % 2, :].rearrange("p (c m) -> p c m", c=DC), halved(6 + d % 2),
                   rc[:, d, :].unsqueeze(1).to_broadcast([P, DC, D]), ALU.mult).then_inc(agg_ok, 1)

            def relu(s):
                wait(relu_hi, "relu")
                low(0, relu_lo)

            def gates(s):
                r, z, n = hf[:, 1, :], hf[:, 0, :], flat(res[:, s, :, :])
                wait(gate_act, "gates", 6, 2)
                stt(r, r, 1.0, n, ALU.add, ALU.mult).then_inc(pre_ok, 1)
                wait(pre_ok, "gates", 2, 1)
                wait(out_mm, "gates_out", 3)
                tt(r, bank[:, 4, :], r, ALU.add).then_inc(pre_ok, 1)
                wait(cand_ok, "gates", 2)
                tt(r, f32(flat(tTh[:, 0, :, :])), n, ALU.subtract).then_inc(mix_ok, 1)
                wait(mix_ok, "gates", 4, 3)
                tt(r, r, f32(flat(tTl[:, 0, :, :])), ALU.add).then_inc(mix_ok, 1)
                wait(mix_ok, "gates", 4, 2)
                stt(r, z, 1.0, r, ALU.add, ALU.mult).then_inc(mix_ok, 1)
                wait(mix_ok, "gates", 4, 1)
                stt(flat(y[:, s, :, :]), r, 0.5, n, ALU.mult, ALU.add).then_inc(mix_ok, 1)

            walk(e, t, {"keeps": keeps, "stats": stats, "centre": centre, "norm": norm, "turn": turn, "qk": qk,
                        "score": score, "heads": heads, "proj": proj, "mlp_sum": mlp_sum, "a2": a2, "score2": score2,
                        "z2": z2, "hidden": hidden, "masks": masks, "count": count, "agg": agg, "relu": relu,
                        "up": up, "agg_low": agg_low, "gates": gates})

        @block.tensor
        def _(e):
            t = Tally(loops)
            wait = waiter(e, t)

            def mm3(dst, left, right, first=True, last=True, shared=False):
                (lh, ll), (rh, rl) = left, right
                e.matmul(dst, lh, rh, start=first, stop=False, skip_group_check=shared)
                e.matmul(dst, lh, rl, start=False, stop=False, skip_group_check=shared)
                return e.matmul(dst, ll, rh, start=False, stop=last, skip_group_check=shared)

            def w2(name, c, lo, n):
                return wt(WH, name, c, lo, lo + n), wt(WL, name, c, lo, lo + n)

            def tT(c, lo=0, n=D, new=0):
                return tTh[:, new, c, lo:lo + n], tTl[:, new, c, lo:lo + n]

            def by_feature(b, name, m, first=True, last=True, shared=False, new=0):
                for c in range(DC):
                    ins = mm3(halved(b)[:, m, :], w2(name, c, m * P, P), tT(c, new=new), first and c == 0,
                              last and c == DC - 1, shared)
                return ins

            def by_row(b, name, new=0):
                for r in range(RT):
                    for c in range(DC):
                        ins = mm3(halved(b)[:, r, :], tT(c, r * P, P, new), w2(name, c, 0, D), c == 0, c == DC - 1)
                return ins

            def staged(block, c, lo, n, width=D):
                a = block * D + c * width + lo
                return stage[:, a:a + n]

            e.wait_ge(s_vecs, 32)
            e.wait_ge(s_staged, 16)
            for n in range(3):
                for m in range(DC):
                    for c in range(DC):
                        ins = e.matmul(bank[:, 4, DC * n + m:DC * n + m + 1], staged(DC * n, c, m * P, P), col("ln1_b", c),
                                       start=c == 0, stop=c == DC - 1)
            ins.then_inc(s_fold, 1)
            e.wait_ge(s_vb, DC)
            for c in range(DC):
                ins = e.matmul(bank[:, 5, 0:D], vb[:, c, :], staged(3 * DC, c, 0, D), start=c == 0, stop=c == DC - 1)
            ins.then_inc(s_fold, 1)
            e.wait_ge(s_staged, 32)
            for f in range(FF // P):
                for c in range(DC):
                    ins = e.matmul(bank[:, 6, f:f + 1], staged(0, c, f * P, P, FF), col("ln2_b", c),
                                   start=c == 0, stop=c == DC - 1)
            ins.then_inc(s_fold, 1)
            e.wait_ge(s_staged, 64)
            e.wait_ge(s_vb, 2 * DC)
            for c in range(DC):
                ins = e.matmul(bank[:, 7, 0:D], vb[:, c, :], staged(3 * DC, c, 0, D), start=c == 0, stop=c == DC - 1)
            ins.then_inc(s_fold, 1)
            e.wait_ge(s_staged, 16 * len(GROUPS))
            e.wait_ge(s_scaled, len(SCALED))
            for n in range(2):
                for m in range(DC):
                    for c in range(DC):
                        ins = e.matmul(halved(4 + n)[:, m, :], staged(2 * DC * n, c, m * P, P), staged(2 * DC * n + DC, c, 0, D),
                                       start=c == 0, stop=c == DC - 1)
                ins.then_inc(s_prod, 1)
            e.wait_ge(s_wlo, len(GROUPS) + 1)
            e.wait_ge(s_ident, 1)

            def turn(s, src):
                rows = y if src in ("sum", "z2") else nx
                if src == "heads":
                    wait(heads_ok, "heads")
                elif src in ("norm", "in"):
                    wait(norm_ok, "norm", 2)
                elif src == "sum":
                    wait(sum_ok, "mlp_sum")
                else:
                    wait(z2_ok, "z2", 2)
                if src == "in" and t.i is not None:
                    wait(relu_ok, "relu", 2)
                for c in range(DC):
                    for r in range(RT):
                        ins = e.transpose(halved(4)[:, c, r * P:r * P + P], rows[:, s, r, c * P:c * P + P], ident[:, :])
                ins.then_inc(turn_mm, 1)

            def qk(s, a):
                wait(turn_lo, "turn")
                if a == 0 and t.i is not None:
                    wait(gate_act, "gates", 6)
                for b, name in ((5, "q%d" % a), (6, "k%d" % a)):
                    for m in range(DC):
                        ins = by_feature(b, name, m, new=int(a == 0))
                    ins.then_inc(qk_mm, 1)

            def v(s, a):
                by_row(7, "v%d" % a, int(a == 0)).then_inc(v_mm, 1)

            def score(s, a, h):
                c, p = h // HPC, h % HPC * HD
                if h == 0:
                    wait(qk_lo, "qk", 4)
                if h >= 2:
                    wait(score_max, "score", 2, 4)
                for r in range(RT):
                    ins = mm3(halved(h % 2)[:, r, :],
                              (qh[p:p + HD, s, c, r * P:r * P + P], ql[p:p + HD, s, c, r * P:r * P + P]),
                              (kh[p:p + HD, s, c, :], kl[p:p + HD, s, c, :]))
                ins.then_inc(score_mm, 1)

            def turn_p(s, a, h):
                wait(prob_ok, "score", 2, 2 * (min(h + 2, H - 1) - h))
                if h >= 1:
                    wait(turn_p_ok, "turn_p", 1, 1)
                for k in range(DC):
                    for r in range(RT):
                        ins = e.transpose(halved(2)[:, k, r * P:r * P + P], S[:, h % SLOTS, r, k * P:k * P + P], ident[:, :])
                ins.then_inc(turn_p_mm, 1)

            def pv(s, a, h):
                if h == 0:
                    wait(v_ok, "v")
                wait(turn_p_ok, "turn_p", 1, 1 if h + 1 < H else 0)
                for r in range(RT):
                    for k in range(DC):
                        ins = e.matmul(halved(3)[:, r, h * HD:h * HD + HD], PT[:, h % 2, k, r * P:r * P + P],
                                       V[:, s, k, h * HD:h * HD + HD], start=k == 0, stop=k == DC - 1)
                ins.then_inc(pv_mm, 1)

            def proj(s, name):
                wait(turn_lo, "turn")
                by_row(5, name).then_inc(proj_mm, 1)

            def up(s, j):
                wait(turn_lo, "turn")
                if j >= 2:
                    wait(up_act, "up", 2, 4)
                for f in range(2):
                    for c in range(DC):
                        ins = mm3(halved(6 + j % 2)[:, f, :], w2("w1", c, (2 * j + f) * P, P), tT(c), c == 0, c == DC - 1)
                ins.then_inc(up_mm, 1)

            def down(s, j):
                wait(up_lo, "up", 1, min(j + 2, UPS - 1) - j)
                for f in range(2):
                    for r in range(RT):
                        at = f * D + r * P
                        ins = mm3(halved(5)[:, r, :], (hh[:, j % 2, at:at + P], hl[:, j % 2, at:at + P]),
                                  w2("w2", 2 * j + f, 0, D), (j, f, r) == (0, 0, 0), (j, f) == (UPS - 1, 1), True)
                ins.then_inc(down_mm, 1)

            def a2(s):
                wait(turn_lo, "turn")
                for m in range(DC):
                    ins = by_feature(5, "qk2", m)
                ins.then_inc(a2_mm, 1)

            def score2(s):
                wait(a2_lo, "a2")
                for r in range(RT):
                    for c in range(DC):
                        ins = mm3(halved(6)[:, r, :], (kh[:, s, c, r * P:r * P + P], kl[:, s, c, r * P:r * P + P]), tT(c),
                                  c == 0, c == DC - 1)
                ins.then_inc(score2_mm, 1)

            def turn_p2(s):
                wait(prob2_ok, "score2", 2)
                for k in range(DC):
                    for r in range(RT):
                        ins = e.transpose(halved(7)[:, k, r * P:r * P + P], hf[:, 0, r * D + k * P:r * D + k * P + P], ident[:, :])
                ins.then_inc(turn_p2_mm, 1)

            def z2(s):
                wait(turn_p2_ok, "turn_p2")
                for r in range(RT):
                    for k in range(DC):
                        ins = e.matmul(halved(5)[:, r, :], hf[:, 1, k * D + r * P:k * D + r * P + P], nx[:, s, k, :],
                                       start=k == 0, stop=k == DC - 1)
                ins.then_inc(z2_mm, 1)

            def turn_adj(s):
                wait(v_ok, "v")
                if t.i is None and s:
                    wait(gate_act, "gates", 6)
                for k in range(DC):
                    for r in range(RT):
                        ins = e.transpose(halved(7)[:, k, r * P:r * P + P], adjf[s][:, r, k * P:k * P + P], ident[:, :])
                ins.then_inc(adjT_mm, 1)

            def count(s):
                wait(mask_ok, "masks", LABELS)
                for l in range(LABELS):
                    for r in range(RT):
                        at = (l * RT + r) * CW
                        for k in range(DC):
                            ins = e.matmul(bank[:, 4, at:at + CW], mask[s][l][:, k, r * P:r * P + P], ones_r[:, :],
                                           start=k == 0, stop=k == DC - 1)
                ins.then_inc(cnt_mm, 1)

            def spread(s, p):
                wait(rcol_ok, "count")
                for n in range(2 * RT):
                    ins = e.transpose(bank[:, 6 + p, n * P:n * P + P], rspread[s][p][:, n, :], ident[:, :])
                ins.then_inc(spread_mm, 1)

            def agg(s, d):
                if d == 0:
                    wait(spread_ok, "spread")
                wait(hid_lo, "hidden")
                if d >= 2:
                    wait(agg_ok, "agg", 1, 2)
                for c in range(DC):
                    for k in range(DC):
                        for n, half in enumerate((hidh[s], hidl[s])):
                            ins = e.matmul(halved(6 + d % 2)[:, c, :], half[:, k, c * P:c * P + P], mask[s][d][:, k, :],
                                           start=(k, n) == (0, 0), stop=(k, n) == (DC - 1, 1))
                ins.then_inc(agg_mm, 1)

            def wd(s, d):
                wait(agg_lo, "agg_low")
                for c in range(DC):
                    for m in range(DC):
                        ins = mm3(halved(4)[:, m, :], w2("wd", DC * d + c, m * P, P),
                                  (hh[:, d % 2, c * D:c * D + D], hl[:, d % 2, c * D:c * D + D]),
                                  (d, c, m) == (0, 0, 0), (d, c) == (LABELS - 1, DC - 1), True)
                ins.then_inc(wd_mm, 1)

            def gates_hid(s, which):
                if which == "r":
                    wait(turn_lo, "turn")
                    for m in range(DC):
                        by_feature(5, "rh", m, first=m == 0, last=False, shared=True)
                else:
                    for m in range(DC):
                        by_feature(6, "zh", m, first=m == 0, last=False, shared=True)
                    for m in range(DC):
                        ins = by_feature(7, "nh", m)
                    ins.then_inc(hid_mm, 1)

            def gates_out(s):
                wait(relu_lo, "relu")
                for b, name, fresh in ((5, "ri", False), (6, "zi", False), (4, "ni", True)):
                    if fresh and t.i is not None:
                        wait(turn_lo, "turn")
                    for m in range(DC):
                        for c in range(DC):
                            ins = mm3(halved(b)[:, m, :], w2(name, c, m * P, P),
                                      (hh[:, 0, c * D:c * D + D], hl[:, 0, c * D:c * D + D]),
                                      fresh and c == 0, c == DC - 1, not fresh)
                    ins.then_inc(out_mm, 1)

            def turn_back(s):
                wait(mix_ok, "gates", 4)
                wait(qk_lo, "qk", 4)
                for r in range(RT):
                    for c in range(DC):
                        ins = e.transpose(halved(6)[:, r, c * P:c * P + P], y[:, s, c, r * P:r * P + P], ident[:, :])
                ins.then_inc(back_mm, 1)

            walk(e, t, {"turn": turn, "qk": qk, "v": v, "score": score, "turn_p": turn_p, "pv": pv, "proj": proj,
                        "up": up, "down": down, "a2": a2, "score2": score2, "turn_p2": turn_p2, "z2": z2,
                        "turn_adj": turn_adj, "count": count, "spread": spread, "agg": agg, "wd": wd, "gates_hid": gates_hid,
                        "gates_out": gates_out, "turn_back": turn_back})


def kernel(**inputs):
    import numpy as _np
    import concourse.bacc as _bacc
    from concourse import mybir as _mybir
    from concourse.bass_utils import run_bass_kernel_spmd as _run

    a = {k: _np.asarray(v) for k, v in inputs.items()}

    def chunks(w):
        return w.reshape(w.shape[0] // P, P, w.shape[1]).transpose(1, 0, 2).reshape(P, -1)

    mats = {"q0": a["L0_gnn_wq"], "k0": a["L0_gnn_wk"], "v0": a["L0_gnn_wv"], "o0": a["L0_gnn_wo"],
            "w1": a["L0_gnn_w1"], "w2": a["L0_gnn_w2"],
            "q1": a["L1_gnn_Wq"], "k1": a["L1_gnn_Wk"], "v1": a["L1_gnn_Wv"], "o1": a["L1_gnn_Wo"],
            "wd": a["L3_gnn_Wd"].T, "ri": a["L3_gnn_Wri"].T, "rh": a["L3_gnn_Wrh"].T, "zi": a["L3_gnn_Wzi"].T,
            "zh": a["L3_gnn_Wzh"].T, "ni": a["L3_gnn_Wni"].T, "nh": a["L3_gnn_Wnh"].T,
            "q2T": a["L2_gnn_Wq"].T, "k2T": a["L2_gnn_Wk"].T, "v2T": a["L2_gnn_Wv"].T, "o2": a["L2_gnn_Wo"]}
    vecs = {"ln1_g": a["L0_gnn_ln1_g"], "ln1_b": a["L0_gnn_ln1_b"], "ln2_g": a["L0_gnn_ln2_g"], "ln2_b": a["L0_gnn_ln2_b"],
            "bq0": a["L0_gnn_bq"], "bk0": a["L0_gnn_bk"], "bv0": a["L0_gnn_bv"],
            "bq1": a["L1_gnn_bq"], "bk1": a["L1_gnn_bk"], "bv1": a["L1_gnn_bv"],
            "bd": a["L3_gnn_bd"], "bri": a["L3_gnn_bri"], "brh": a["L3_gnn_brh"], "bzi": a["L3_gnn_bzi"],
            "bzh": a["L3_gnn_bzh"], "bni": a["L3_gnn_bni"], "bnh": a["L3_gnn_bnh"], "b1": a["L0_gnn_b1"]}
    rowv = {"bo0": a["L0_gnn_bo"], "b2": a["L0_gnn_b2"], "bo1": a["L1_gnn_bo"], "bo2": a["L2_gnn_bo"],
            "g1": a["L1_gnn_gamma"], "be1": a["L1_gnn_beta"], "g2": a["L2_gnn_gamma"], "be2": a["L2_gnn_beta"],
            "g3": a["L3_gnn_gamma"], "be3": a["L3_gnn_beta"]}
    arrays = {
        "x": _np.ascontiguousarray(a["x"]),
        "adj": _np.ascontiguousarray(a["adj"]),
        "weights": _np.concatenate([chunks(mats[n]) for g in GROUPS for n in g], axis=1),
        "cols": _np.ascontiguousarray(_np.concatenate([vecs[n].reshape(-1, P) for n in COLS]).T),
        "rows": _np.ascontiguousarray(_np.broadcast_to(_np.stack([rowv[n] for n in ROWV]), (P, len(ROWV), D))),
    }
    nc = _bacc.Bacc("TRN2", target_bir_lowering=False, num_devices=1)
    args = [nc.dram_tensor(n, v.shape, _mybir.dt.from_np(v.dtype), kind="ExternalInput").ap() for n, v in arrays.items()]
    args.append(nc.dram_tensor("out", a["x"].shape, _mybir.dt.float32, kind="ExternalOutput").ap())
    build(nc, *args)
    r = _run(nc, [arrays], core_ids=[0])
    return r.results[0]["out"]
```

```python
from contextlib import ExitStack

import numpy as np

import concourse.bass as bass
from concourse import mybir

F32 = mybir.dt.float32
F32R = mybir.dt.float32r
I32 = mybir.dt.int32
ALU = mybir.AluOpType
ACT = mybir.ActivationFunctionType

P = 128
D = 256
DC = D // P
RT = D // P
W = RT * D
H = 8
HD = D // H
HPC = P // HD
FF = 4 * D
UPS = FF // P // 2
LABELS = 4
SLOTS = 3
CW = 2
BIG = 1e38
QSCALE = float(1.0 / np.sqrt(HD))
LN_EPS = 1e-5
AGG_EPS = 1e-8

GROUPS = [["q0", "k0", "v0", "o0"], ["w1"], ["w2"], ["q1", "k1", "v1", "o1"],
          ["wd"], ["ri", "rh", "zi", "zh"], ["ni", "nh"], ["q2T", "k2T", "v2T", "o2"]]
WIDE = {"w1": 8, "w2": 8, "wd": 8}
NBLOCK = 0
WAT = {}
for _g in GROUPS[:-1]:
    for _n in _g:
        WAT[_n] = NBLOCK
        NBLOCK += WIDE.get(_n, DC)
WAT["qk2"], WAT["vo2"] = NBLOCK, NBLOCK + DC
NBLOCK += 2 * DC

SCALED = [0, 1, 3, 6, 7]
COLS = ["ln1_g", "ln1_b", "ln2_g", "ln2_b", "bq0", "bk0", "bv0", "bq1", "bk1", "bv1",
        "bd", "bri", "brh", "bzi", "bzh", "bni", "bnh", "b1"]
CAT = {n: DC * j for j, n in enumerate(COLS)}
NCOL = DC * (len(COLS) - 1) + FF // P
ROWV = ["bo0", "b2", "bo1", "bo2", "g1", "be1", "g2", "be2", "g3", "be3"]
RAT = {n: j for j, n in enumerate(ROWV)}
BAT = {"q0": 0, "k0": 2, "v0": 4, "q1": 6, "r": 8, "z": 10, "nh": 12, "b1": 14}



def attention(s, a):
    steps = []
    for t in range(H + 3):
        if 2 <= t <= H + 1:
            steps.append(("turn_p", s, a, t - 2))
        if t < H:
            steps.append(("score", s, a, t))
        if t >= 3:
            steps.append(("pv", s, a, t - 3))
    return steps + [("heads", s, a)]


def before(s):
    return [("stats", s, "in"), "*", "*", ("norm", s, "in"), ("prep", s), ("residual", s, "in"), "*",
            ("turn", s, "in"), "*", "*", ("qk", s, 0), ("v", s, 0)]


def middle(s):
    return [
        ("turn", s, "heads"), *"**", ("proj", s, "o0"), *"**", ("stats", s, "mid"), *"**", "back", *"**",
        ("norm", s, "mid"), "*", "stats", ("turn", s, "norm"), "*", "centre", *"**", ("keeps", s), *"****",
        ("residual", s, "mid"), ("up", s, 0), "*", ("up", s, 1), ("up", s, 2), ("down", s, 0), ("up", s, 3),
        ("down", s, 1), "*", ("down", s, 2), ("down", s, 3), "*", ("mlp_sum", s), "norm", "*",
        ("turn", s, "sum"), *"*****", ("residual", s, "x2"), ("qk", s, 1), ("v", s, 1)]


def late(s, nxt):
    steps = [
        ("turn_adj", s), ("turn", s, "heads"), *"**", ("proj", s, "o1"), "*", ("stats", s, "l1"), "*",
        ("centre", s, "l1"), "*", "back", ("norm", s, "l1"), "*", ("residual", s, "l1"), "*", "stats",
        ("turn", s, "norm"), "centre", "*", "norm", "*", ("a2", s), *"**", ("score2", s), "*", ("masks", s),
        *"***", ("load_adj", s, 1), ("turn_p2", s), ("count", s), "*", ("z2", s), ("prep", s), "*",
        ("spread", s, 0), ("turn", s, "z2"), *"**", ("proj", s, "vo2"), *"**", ("stats", s, "l2"), "*",
        ("spread", s, 1), ("load_x", s, 1), ("centre", s, "l2"), ("norm", s, "l2"), ("hidden", s),
        ("turn", s, "norm"), "*", ("agg", s, 0), ("agg", s, 1), ("agg_low", s, 0), "*", ("agg_low", s, 1),
        ("wd", s, 0), ("agg", s, 2), ("wd", s, 1), ("agg_low", s, 2), ("agg", s, 3), ("gates_hid", s, "r"),
        ("wd", s, 2), ("agg_low", s, 3), ("wd", s, 3), "*", ("stats", s, "in"), ("norm", s, "in"), ("relu", s),
        ("gates_hid", s, "zn"), ("turn", s, "in"), ("gates_out", s), ("gates", s), ("qk", s, 0),
        ("residual", s, "in"), ("v", s, 0)]
    return [step for step in steps if nxt or not is_next(step)]


def is_next(step):
    return step[0] in ("load_adj", "load_x", "prep", "qk", "v") or step[-1] == "in"


def after(s, lin):
    last = {"back": [("turn_back", s)], "stats": [("stats", s, "fin")], "centre": [("centre", s, "fin")],
            "norm": [("norm", s, "fin"), ("store", s)]}
    return [step for one in lin for step in (last[one] if one in last else [one])]


def first(lin):
    return [step for step in lin if step not in ("back", "stats", "centre", "norm")]


def slot(att, lin):
    att, out = list(att), []
    for step in lin:
        if step != "*":
            out.append(step)
        elif att:
            out.append(att.pop(0))
    return out + att


PROLOGUE = ([("load_adj", 0, 0), ("load_x", 0, 0), ("load_adj", 1, 0), ("load_x", 1, 0)] + slot([], before(0))
            + slot(attention(0, 0), before(1)) + slot(attention(1, 0), first(middle(0)))
            + slot(attention(0, 1), first(middle(1))))
BODY = (slot(attention(1, 1), first(late(0, True))) + slot(attention(0, 0), after(0, late(1, True)))
        + slot(attention(1, 0), after(1, middle(0))) + slot(attention(0, 1), first(middle(1))))
EPILOGUE = (slot(attention(1, 1), first(late(0, False))) + slot([], after(0, late(1, False)))
            + after(1, ["back", "stats", "centre", "norm"]))


class Tally:

    def __init__(self, loops):
        self.loops, self.i, self.base, self.rate, self.here = loops, None, {}, {}, {}
        for step in BODY:
            self.rate[step[0]] = self.rate.get(step[0], 0) + 1
            self.rate[step[:2]] = self.rate.get(step[:2], 0) + 1

    def enter(self, step):
        for key in (step[0], step[:2]):
            self.here[key] = self.here.get(key, 0) + 1

    def loop_begins(self, i):
        self.base, self.here, self.i = self.here, {}, i

    def loop_ends(self):
        self.i = None
        keys = set(self.rate) | set(self.base)
        self.here = {k: self.base.get(k, 0) + self.loops * self.rate.get(k, 0) for k in keys}
        self.base = {}

    def recent(self, key):
        return bool(self.here.get(key))

    def value(self, key, per, less):
        n = per * (self.base.get(key, 0) + self.here.get(key, 0)) - less
        if self.i is None or not self.rate.get(key):
            return n
        return self.i * (per * self.rate[key]) + n


def build(nc, x, adj, weights, cols, rows, out):
    loops = x.shape[0] // 2 - 1
    x_v = x.rearrange("b (q p) d -> b p q d", p=P)
    adj_v = adj.rearrange("b (q p) k -> b p q k", p=P)
    out_v = out.rearrange("b (q p) d -> b p q d", p=P)

    with ExitStack() as ctx:
        def sb(name, shape, dt=F32):
            return ctx.enter_context(nc.sbuf_tensor(name, shape, dt))

        def sem(name):
            return ctx.enter_context(nc.semaphore(name))

        WH = sb("WH", [P, NBLOCK, D], F32R)
        WL = sb("WL", [P, NBLOCK, D], F32R)
        colv = sb("colv", [P, NCOL])
        rowv = sb("rowv", [P, len(ROWV), D])
        bias = sb("bias", [P, 14 + FF // P])
        halves = sb("halves", [P, 2 * DC])
        power = sb("power", [P, RT])
        spare = sb("spare", [P, 1])
        ident = sb("ident", [P, P])
        ones = sb("ones", [P, P])
        ones_r = sb("ones_r", [P, CW], F32R)
        xin = sb("xin", [P, 2, RT, D])
        adjb = sb("adjb", [P, 2, RT, D], I32)
        nb = sb("nb", [P, 2, 2, W])
        res_y = sb("res_y", [P, 2, 2, RT, D])
        res, y = res_y[:, 0], res_y[:, 1]
        nx = sb("nx", [P, 2, RT, D])
        qh = sb("qh", [P, 2, DC, D], F32R)
        ql = sb("ql", [P, 2, DC, D], F32R)
        kh = sb("kh", [P, 2, DC, D], F32R)
        kl = sb("kl", [P, 2, DC, D], F32R)
        V = sb("V", [P, 2, RT, D])
        keep = sb("keep", [P, 2, RT])
        tTh = sb("tTh", [P, 2, DC, D], F32R)
        tTl = sb("tTl", [P, 2, DC, D], F32R)
        hf = sb("hf", [P, 2, W])
        hh = sb("hh", [P, 2, W], F32R)
        hl = sb("hl", [P, 2, W], F32R)
        rc = sb("rc", [P, LABELS, D])
        rcnt = sb("rcnt", [P, LABELS * RT])
        st = sb("st", [P, RT, 6])
        mv = sb("mv", [P, 2, RT, 2])
        rstd = sb("rstd", [P, 2, RT])
        nmax2 = sb("nmax2", [P, RT])
        rsum2 = sb("rsum2", [P, RT])
        rec2 = sb("rec2", [P, RT])
        S = sb("S", [P, SLOTS, RT, D])
        PT = sb("PT", [P, 2, DC, D])
        nmax = sb("nmax", [P, SLOTS, RT])
        rsum = sb("rsum", [P, RT, H])
        rec = sb("rec", [P, RT, H])
        bank = ctx.enter_context(nc.psum_tensor("bank", [P, 8, W], F32))

        def halved(b):
            return bank[:, b, :].rearrange("p (c n) -> p c n", c=2)

        def flat(ap):
            return ap.rearrange("p a b -> p (a b)")

        def f32(ap):
            return ap.bitcast(F32)

        stages = [nb[:, :, :, :].rearrange("p a b c -> p (a b c)"), res_y[:, :, :, :, :].rearrange("p a b c d -> p (a b c d)")]
        nbias = [[nb[:, s, a, :].rearrange("p (r k) -> p r k", r=RT) for a in range(2)] for s in range(2)]
        adjf = [f32(adjb[:, s, :, :]) for s in range(2)]
        adjT = [nbias[s][0] for s in range(2)]
        mask = [[qh[:, s, :, :], ql[:, s, :, :], tTh[:, 1, :, :], tTl[:, 1, :, :]] for s in range(2)]
        rspread = [[buf[:, s, :, :].rearrange("p r (n m) -> p (r n) m", m=P) for buf in (V, xin)] for s in range(2)]
        vb = S[:, 0, :, 0:P]
        hidh = [kh[:, s, :, :] for s in range(2)]
        hidl = [kl[:, s, :, :] for s in range(2)]

        def wt(half, name, c, lo, hi):
            n = FF // D if name == "w1" else 1
            a = WAT[name] + c * n
            return half[:, a:a + n, :].rearrange("p b d -> p (b d)")[:, lo:hi]

        def col(name, c=0):
            return colv[:, CAT[name] + c:CAT[name] + c + 1]

        def bcol(name, c=0):
            return bias[:, BAT[name] + c:BAT[name] + c + 1]

        def row(name):
            return rowv[:, RAT[name], :]

        s_ident0, s_ident, s_const = sem("s_ident0"), sem("s_ident"), sem("s_const")
        waited = sem("waited")
        s_vecs, s_staged = sem("s_vecs"), [sem("s_staged0"), sem("s_staged1")]
        s_fold, s_bias, s_scaled = sem("s_fold"), sem("s_bias"), sem("s_scaled")
        s_whi, s_wlo, s_prod, s_vb, s_rowfix = sem("s_whi"), sem("s_wlo"), sem("s_prod"), sem("s_vb"), sem("s_rowfix")
        x_in = [sem("x_in0"), sem("x_in1")]
        adj_in = [sem("adj_in0"), sem("adj_in1")]
        stored = [sem("stored0"), sem("stored1")]
        mask_bias = sem("mask_bias")
        prep_step = sem("prep_step")
        keep_ok = sem("keep_ok")
        stat_ok = sem("stat_ok")
        mean_ok = sem("mean_ok")
        var_ok = sem("var_ok")
        rstd_ok = sem("rstd_ok")
        cent_ok = sem("cent_ok")
        norm_ok = sem("norm_ok")
        res_ok = sem("res_ok")
        turn_mm = sem("turn_mm")
        turn_hi, turn_lo = sem("turn_hi"), sem("turn_lo")
        qk_mm = sem("qk_mm")
        qk_hi, qk_lo = sem("qk_hi"), sem("qk_lo")
        v_mm, v_ok = sem("v_mm"), sem("v_ok")
        score_mm = sem("score_mm")
        score_max = sem("score_max")
        prob_ok = sem("prob_ok")
        turn_p_mm, turn_p_ok = sem("turn_p_mm"), sem("turn_p_ok")
        pv_mm = sem("pv_mm")
        rec_ok, heads_ok = sem("rec_ok"), sem("heads_ok")
        proj_mm, proj_ok = sem("proj_mm"), sem("proj_ok")
        up_mm = sem("up_mm")
        up_act = sem("up_act")
        up_hi, up_lo = sem("up_hi"), sem("up_lo")
        down_mm, sum_ok = sem("down_mm"), sem("sum_ok")
        a2_mm, a2_hi, a2_lo = sem("a2_mm"), sem("a2_hi"), sem("a2_lo")
        score2_mm = sem("score2_mm")
        score2_max, prob2_ok = sem("score2_max"), sem("prob2_ok")
        turn_p2_mm, turn_p2_ok = sem("turn_p2_mm"), sem("turn_p2_ok")
        z2_mm, rec2_ok, z2_ok = sem("z2_mm"), sem("rec2_ok"), sem("z2_ok")
        hid_hi, hid_lo = sem("hid_hi"), sem("hid_lo")
        adjT_mm, adjT_ok = sem("adjT_mm"), sem("adjT_ok")
        mask_ok = sem("mask_ok")
        table_in = sem("table_in")
        cnt_mm, cnt_eps, rc_ok, rcol_ok = sem("cnt_mm"), sem("cnt_eps"), sem("rc_ok"), sem("rcol_ok")
        spread_mm, spread_ok = sem("spread_mm"), sem("spread_ok")
        agg_mm, agg_ok, agg_hi, agg_lo = sem("agg_mm"), sem("agg_ok"), sem("agg_hi"), sem("agg_lo")
        wd_mm = sem("wd_mm")
        relu_ok = sem("relu_ok")
        relu_hi, relu_lo = sem("relu_hi"), sem("relu_lo")
        hid_mm, out_mm = sem("hid_mm"), sem("out_mm")
        gate_act = sem("gate_act")
        pre_ok = sem("pre_ok")
        cand_ok = sem("cand_ok")
        mix_ok = sem("mix_ok")
        back_mm = sem("back_mm")

        block = ctx.enter_context(nc.Block())

        def walk(e, tally, ops):
            def run(steps):
                for step in steps:
                    tally.enter(step)
                    if step[0] in ops:
                        ops[step[0]](*step[1:])

            run(PROLOGUE)
            with e.Fori(0, loops) as i:
                tally.loop_begins(i)
                run(BODY)
            tally.loop_ends()
            run(EPILOGUE)

        def waiter(e, tally):
            def wait(s, key, per=1, less=0, alone=False):
                ins = e.wait_ge(s, tally.value(key, per, less))
                if alone:
                    ins.then_inc(waited, 1)
            return wait

        def group_span(j):
            return WAT[GROUPS[j][0]], sum(WIDE.get(n, DC) for n in GROUPS[j])

        @block.sync
        def _(e):
            t = Tally(loops)
            wait = waiter(e, t)
            e.dma_start(colv[:, :], cols).then_inc(s_vecs, 16)
            e.dma_start(rowv[:, :, :], rows).then_inc(s_vecs, 16)
            at = 0
            for j, names in enumerate(GROUPS):
                n = sum(WIDE.get(m, DC) for m in names) * D
                if j >= 2:
                    e.wait_ge(s_wlo, j - 1)
                e.dma_start(stages[j % 2][:, 0:n], weights[:, at:at + n]).then_inc(s_staged[j % 2], 16)
                at += n

            def load_adj(s, ahead):
                g = s if t.i is None else t.i * 2 + (2 * ahead + s)
                if ahead:
                    wait(adjT_mm, "turn_adj", alone=True)
                e.dma_start(adjb[:, s, :, :], adj_v[bass.ds(g, 1), :, :, :].rearrange("a p r d -> (a p) r d")).then_inc(adj_in[s], 16)

            def load_x(s, ahead):
                g = s if t.i is None else t.i * 2 + (2 * ahead + s)
                if ahead:
                    wait(turn_hi, "turn", alone=True)
                    wait(res_ok, "residual", alone=True)
                    wait(spread_mm, "spread", alone=True)
                e.dma_start(xin[:, s, :, :], x_v[bass.ds(g, 1), :, :, :].rearrange("a p r d -> (a p) r d")).then_inc(x_in[s], 16)

            def store(s):
                g = 2 * loops + s if t.i is None else t.i * 2 + s
                wait(norm_ok, "norm", 2, alone=True)
                e.dma_start(out_v[bass.ds(g, 1), :, :, :].rearrange("a p r d -> (a p) r d"), y[:, s, :, :]).then_inc(stored[s], 16)

            walk(e, t, {"load_adj": load_adj, "load_x": load_x, "store": store})
            for s in range(2):
                wait(stored[s], ("store", s), 16)

        @block.gpsimd
        def _(e):
            t = Tally(loops)
            wait = waiter(e, t)
            e.memset(ident[:, :], 0.0).then_inc(s_ident0, 1)
            e.memset(power[:, :], -0.5).then_inc(s_const, 1)
            e.memset(ones[:, :], 1.0).then_inc(s_const, 1)
            e.wait_ge(s_ident0, 1)
            e.affine_select(out=ident[:, :], in_=ident[:, :], compare_op=ALU.not_equal, fill=1.0,
                            base=0, pattern=[[-1, P]], channel_multiplier=1).then_inc(s_ident, 1)
            e.wait_ge(s_const, 2)
            e.wait_ge(s_rowfix, 2)

            def stats(s, which):
                wait(var_ok, "stats")
                e.tensor_tensor(rstd[:, s, :], rstd[:, s, :], power[:, :], ALU.pow).then_inc(rstd_ok, 1)

            def prep(s):
                f, n0, n1 = flat(adjf[s]), nb[:, s, 0, :], nb[:, s, 1, :]
                if t.i is not None:
                    wait(mask_ok, "masks", LABELS)
                    wait(score2_max, "score2", 2)
                wait(adj_in[s], ("load_adj", s), 16, alone=True)
                e.tensor_copy(f, flat(adjb[:, s, :, :])).then_inc(mask_bias, 1)
                wait(mask_bias, "prep", 4, 3, alone=True)
                e.tensor_scalar(n0, f, -0.1, 1.0, ALU.mult, ALU.mult).then_inc(prep_step, 1)
                e.tensor_scalar(n1, f, 0.0, BIG, ALU.is_le, ALU.mult).then_inc(prep_step, 1)
                wait(prep_step, "prep", 3, 1)
                e.tensor_tensor(n0, n0, f, ALU.mult).then_inc(prep_step, 1)
                wait(prep_step, "prep", 3)
                e.tensor_tensor(n0, n0, n1, ALU.add).then_inc(mask_bias, 1)
                wait(mask_bias, "prep", 4, 2, alone=True)
                e.tensor_scalar(n1, f, 0.0, BIG, ALU.is_equal, ALU.mult).then_inc(mask_bias, 2)

            def residual(s, which):
                src, name = {"in": (xin, "bo0"), "mid": (y, "b2"), "x2": (y, "bo1"), "l1": (nx, "bo2")}[which]
                if which == "in":
                    wait(x_in[s], ("load_x", s), 16)
                    if t.i is not None:
                        wait(mix_ok, "gates", 5)
                elif which == "mid":
                    wait(proj_ok, "proj")
                elif which == "x2":
                    wait(sum_ok, "mlp_sum")
                else:
                    wait(norm_ok, "norm", 2)
                for r in range(RT):
                    op = e.tensor_tensor(res[:, s, r, :], src[:, s, r, :], row(name), ALU.add)
                op.then_inc(res_ok, 1)

            def high(slot, done):
                e.tensor_scalar(hh[:, slot, :], hf[:, slot, :], 1.0, 0.0, ALU.mult, ALU.add).then_inc(done, 1)

            def up(s, j):
                if j >= 2:
                    wait(down_mm, "down", 1, -1)
                wait(up_act, "up", 2, alone=True)
                high(j % 2, up_hi)

            def hidden(s):
                wait(norm_ok, "norm", 2, alone=True)
                e.tensor_scalar(flat(hidh[s]), flat(nx[:, s, :, :]), 1.0, 0.0, ALU.mult, ALU.add).then_inc(hid_hi, 1)

            def agg(s, d):
                if d >= 2:
                    wait(wd_mm, "wd")
                wait(agg_ok, "agg", alone=True)
                high(d % 2, agg_hi)

            def relu(s):
                wait(relu_ok, "relu", 2, alone=True)
                high(0, relu_hi)

            def gates(s):
                mix, z, n = flat(y[:, s, :, :]), hf[:, 0, :], flat(res[:, s, :, :])
                e.tensor_tensor(mix, f32(flat(tTh[:, 0, :, :])), f32(flat(tTl[:, 0, :, :])), ALU.add).then_inc(mix_ok, 1)
                wait(gate_act, "gates", 6, alone=True)
                e.tensor_scalar(z, z, 0.5, 0.5, ALU.mult, ALU.add).then_inc(mix_ok, 1)
                wait(cand_ok, "gates", 2)
                wait(mix_ok, "gates", 5, 3)
                e.tensor_tensor(mix, mix, n, ALU.subtract).then_inc(mix_ok, 1)
                wait(mix_ok, "gates", 5, 2)
                e.tensor_tensor(mix, mix, z, ALU.mult).then_inc(mix_ok, 1)
                wait(mix_ok, "gates", 5, 1)
                e.tensor_tensor(mix, mix, n, ALU.add).then_inc(mix_ok, 1)

            walk(e, t, {"prep": prep, "stats": stats, "residual": residual, "up": up, "hidden": hidden, "agg": agg,
                        "relu": relu, "gates": gates})

        @block.scalar
        def _(e):
            t = Tally(loops)
            wait = waiter(e, t)
            for j in range(len(GROUPS) - 1):
                a, n = group_span(j)
                e.wait_ge(s_staged[j % 2], 16 * (j // 2 + 1))
                if j in SCALED:
                    e.wait_ge(s_scaled, SCALED.index(j) + 1)
                e.activation(flat(WH[:, a:a + n, :]), stages[j % 2][:, 0:n * D], ACT.Copy).then_inc(s_whi, 1)
            for j, name in enumerate(("qk2", "vo2")):
                e.wait_ge(s_prod, j + 1)
                e.activation(flat(WH[:, WAT[name]:WAT[name] + DC, :]), bank[:, 4 + j, :], ACT.Copy).then_inc(s_whi, 1)

            def copy(dst, src, done):
                e.activation(dst, src, ACT.Copy).then_inc(done, 1)

            def turn(s, src):
                wait(turn_mm, "turn")
                copy(flat(tTh[:, int(src == "in"), :, :]), bank[:, 4, :], turn_hi)

            def qk(s, a):
                for n, (dst, b) in enumerate(((qh, 5), (kh, 6))):
                    wait(qk_mm, "qk", 2, 1 - n)
                    for m in range(DC):
                        bc = bcol("q%d" % a, m) if n == 0 else (bcol("k0", m) if a == 0 else col("bk1", m))
                        e.activation(dst[:, s, m, :], halved(b)[:, m, :], ACT.Identity, bias=bc).then_inc(qk_hi, 1)

            def v(s, a):
                wait(v_mm, "v")
                copy(flat(V[:, s, :, :]), bank[:, 7, :], v_ok)

            def score(s, a, h):
                for r in range(RT):
                    wait(score_max, "score", 2, 1 - r)
                    e.activation(S[:, h % SLOTS, r, :], S[:, h % SLOTS, r, :], ACT.Exp, bias=nmax[:, h % SLOTS, r:r + 1],
                                 scale=-1.0, accum_out=rsum[:, r, h:h + 1]).then_inc(prob_ok, 1)

            def turn_p(s, a, h):
                wait(turn_p_mm, "turn_p")
                if h >= 2:
                    wait(pv_mm, "pv")
                copy(flat(PT[:, h % 2, :, :]), bank[:, 2, :], turn_p_ok)

            def up(s, j):
                wait(up_mm, "up")
                if j >= 2:
                    wait(up_lo, "up", 1, 2)
                for f in range(2):
                    e.activation(hf[:, j % 2, f * D:f * D + D], halved(6 + j % 2)[:, f, :], ACT.Gelu,
                                 bias=bcol("b1", 2 * j + f)).then_inc(up_act, 1)

            def mlp_sum(s):
                e.activation(spare[:, :], power[:, 0:1], ACT.Exp).then_inc(table_in, 1)

            def a2(s):
                wait(a2_mm, "a2")
                copy(flat(kh[:, s, :, :]), bank[:, 5, :], a2_hi)

            def score2(s):
                for r in range(RT):
                    wait(score2_max, "score2", 2, 1 - r)
                    e.activation(hf[:, 0, r * D:r * D + D], hf[:, 0, r * D:r * D + D], ACT.Exp, bias=nmax2[:, r:r + 1],
                                 scale=-1.0, accum_out=rsum2[:, r:r + 1]).then_inc(prob2_ok, 1)

            def turn_p2(s):
                wait(turn_p2_mm, "turn_p2")
                copy(hf[:, 1, :], bank[:, 7, :], turn_p2_ok)

            def turn_adj(s):
                wait(adjT_mm, "turn_adj")
                copy(flat(adjT[s]), bank[:, 7, :], adjT_ok)

            def spread(s, p):
                wait(spread_mm, "spread")
                copy(flat(rc[:, 2 * p:2 * p + 2, :]), bank[:, 6 + p, :], spread_ok)

            def relu(s):
                wait(wd_mm, "wd")
                for m in range(DC):
                    e.activation(hf[:, 0, m * D:m * D + D], halved(4)[:, m, :], ACT.Relu, bias=col("bd", m)).then_inc(relu_ok, 1)

            def gates(s):
                wait(hid_mm, "gates_out")
                for m in range(DC):
                    e.activation(res[:, s, m, :], halved(7)[:, m, :], ACT.Identity, bias=bcol("nh", m)).then_inc(gate_act, 1)
                for less, b, name, dst in ((2, 5, "r", hf[:, 1, :]), (1, 6, "z", hf[:, 0, :])):
                    wait(out_mm, "gates_out", 3, less)
                    for m in range(DC):
                        e.activation(dst[:, m * D:m * D + D], halved(b)[:, m, :], ACT.Tanh, bias=bcol(name, m),
                                     scale=0.5).then_inc(gate_act, 1)
                wait(pre_ok, "gates", 2)
                for m in range(DC):
                    e.activation(res[:, s, m, :], hf[:, 1, m * D:m * D + D], ACT.Tanh, bias=col("bni", m)).then_inc(cand_ok, 1)

            walk(e, t, {"turn": turn, "qk": qk, "v": v, "score": score, "turn_p": turn_p, "up": up, "mlp_sum": mlp_sum, "a2": a2,
                        "score2": score2, "turn_p2": turn_p2, "turn_adj": turn_adj, "spread": spread, "relu": relu,
                        "gates": gates})

        @block.vector
        def _(e):
            t = Tally(loops)
            wait = waiter(e, t)
            tsc, tt, stt = e.tensor_scalar, e.tensor_tensor, e.scalar_tensor_tensor
            e.wait_ge(s_vecs, 32)
            e.wait_ge(s_const, 2)
            tt(halves[:, 0:DC], colv[:, CAT["bri"]:CAT["bri"] + DC], colv[:, CAT["brh"]:CAT["brh"] + DC], ALU.add).then_inc(s_bias, 1)
            tt(halves[:, DC:2 * DC], colv[:, CAT["bzi"]:CAT["bzi"] + DC], colv[:, CAT["bzh"]:CAT["bzh"] + DC], ALU.add).then_inc(s_bias, 1)
            e.wait_ge(s_bias, 2)
            tsc(bias[:, BAT["r"]:BAT["r"] + 2 * DC], halves[:, :], 0.5, None, ALU.mult).then_inc(s_bias, 1)
            tsc(bias[:, BAT["nh"]:BAT["nh"] + DC], colv[:, CAT["bnh"]:CAT["bnh"] + DC], 0.5, None, ALU.mult).then_inc(s_bias, 1)
            tsc(bias[:, BAT["q1"]:BAT["q1"] + DC], colv[:, CAT["bq1"]:CAT["bq1"] + DC], -QSCALE, None, ALU.mult).then_inc(s_bias, 1)
            tsc(ones_r[:, :], ones[:, 0:CW], 1.0, None, ALU.mult).then_inc(s_bias, 1)

            def spread_vector(src):
                for c in range(DC):
                    tsc(vb[:, c, :], ones[:, :], src(c), None, ALU.mult).then_inc(s_vb, 1)

            def scale(j, lo, n, by, const):
                part = stages[j % 2][:, lo:lo + n]
                if by is None:
                    return tsc(part, part, const, None, ALU.mult)
                return tsc(part, part, by, const, ALU.mult, ALU.mult)

            def split_low(j, a, n, src):
                e.wait_ge(s_whi, j + 1)
                tt(flat(WL[:, a:a + n, :]), src, f32(flat(WH[:, a:a + n, :])), ALU.subtract).then_inc(s_wlo, 1)

            for j in range(len(GROUPS)):
                e.wait_ge(s_staged[j % 2], 16 * (j // 2 + 1))
                if j == 0:
                    e.wait_ge(s_fold, 1)
                    for n, name in enumerate(("q0", "k0", "v0")):
                        tt(bias[:, BAT[name]:BAT[name] + DC], bank[:, 4, DC * n:DC * n + DC],
                           colv[:, CAT["b" + name]:CAT["b" + name] + DC], ALU.add).then_inc(s_bias, 1)
                    e.wait_ge(s_bias, 9)
                    tsc(bias[:, BAT["q0"]:BAT["q0"] + DC], bias[:, BAT["q0"]:BAT["q0"] + DC], -QSCALE, None, ALU.mult).then_inc(s_bias, 1)
                    spread_vector(lambda c: bcol("v0", c))
                    e.wait_ge(s_fold, 2)
                    tt(row("bo0"), bank[:, 5, 0:D], row("bo0"), ALU.add).then_inc(s_rowfix, 1)
                    for w, const in enumerate((-QSCALE, 1.0, 1.0)):
                        for c in range(DC):
                            ins = scale(j, (DC * w + c) * D, D, col("ln1_g", c), const)
                    ins.then_inc(s_scaled, 1)
                elif j == 1:
                    e.wait_ge(s_fold, 3)
                    tt(bias[:, BAT["b1"]:BAT["b1"] + FF // P], bank[:, 6, 0:FF // P],
                       colv[:, CAT["b1"]:CAT["b1"] + FF // P], ALU.add).then_inc(s_bias, 1)
                    for c in range(DC):
                        ins = scale(j, c * FF, FF, col("ln2_g", c), 1.0)
                    ins.then_inc(s_scaled, 1)
                elif j == 3:
                    spread_vector(lambda c: col("bv1", c))
                    e.wait_ge(s_fold, 4)
                    tt(row("bo1"), bank[:, 7, 0:D], row("bo1"), ALU.add).then_inc(s_rowfix, 1)
                    scale(j, 0, DC * D, None, -QSCALE).then_inc(s_scaled, 1)
                elif j == 6:
                    scale(j, DC * D, DC * D, None, 0.5).then_inc(s_scaled, 1)
                elif j == 7:
                    scale(j, 0, DC * D, None, -1.0 / float(np.sqrt(D))).then_inc(s_scaled, 1)
                if j < len(GROUPS) - 1:
                    a, n = group_span(j)
                    split_low(j, a, n, stages[j % 2][:, 0:n * D])
            for n, name in enumerate(("qk2", "vo2")):
                split_low(len(GROUPS) - 1 + n, WAT[name], DC, bank[:, 4 + n, :])

            def source(s, which):
                return halved(6) if which == "fin" else (xin if which == "in" else y)[:, s, :, :]

            def keeps(s):
                wait(mask_bias, "prep", 4)
                e.tensor_reduce(keep[:, s, :], nbias[s][1], mybir.AxisListType.X, ALU.min).then_inc(keep_ok, 1)
                wait(keep_ok, "keeps", 2, 1)
                tsc(keep[:, s, :], keep[:, s, :], 1.0, None, ALU.is_lt).then_inc(keep_ok, 1)

            def stats(s, which):
                src = source(s, which)
                if which == "in":
                    wait(x_in[s], ("load_x", s), 16)
                elif which == "fin":
                    wait(back_mm, "turn_back")
                else:
                    wait(proj_ok, "proj")
                for r in range(RT):
                    e.bn_stats(st[:, r, :], src[:, r, :]).then_inc(stat_ok, 1)
                for r in range(RT):
                    wait(stat_ok, "stats", 2, 1 - r, alone=True)
                    e.bn_aggr(mv[:, s, r, :], st[:, r, :]).then_inc(mean_ok, 1)
                wait(mean_ok, "stats", 2)
                tsc(rstd[:, s, :], mv[:, s, :, 1], LN_EPS, None, ALU.add).then_inc(var_ok, 1)

            def gains(which):
                n = {"l1": "1", "l2": "2", "fin": "3"}[which]
                return row("g" + n), row("be" + n)

            def centre(s, which):
                src, dst = source(s, which), (y if which == "fin" else nx)
                for r in range(RT):
                    wait(mean_ok, "stats", 2, 1 - r)
                    stt(dst[:, s, r, :], src[:, r, :], mv[:, s, r, 0:1], gains(which)[0], ALU.subtract, ALU.mult).then_inc(cent_ok, 1)

            def norm(s, which):
                wait(rstd_ok, "stats")
                for r in range(RT):
                    if which in ("in", "mid"):
                        tsc(nx[:, s, r, :], source(s, which)[:, r, :], mv[:, s, r, 0:1], rstd[:, s, r:r + 1],
                            ALU.subtract, ALU.mult).then_inc(norm_ok, 1)
                    else:
                        dst = (y if which == "fin" else nx)[:, s, r, :]
                        wait(cent_ok, "centre", 2, 1 - r)
                        stt(dst, dst, rstd[:, s, r:r + 1], gains(which)[1], ALU.mult, ALU.add).then_inc(norm_ok, 1)

            def turn(s, src):
                wait(turn_hi, "turn")
                w = int(src == "in")
                tt(flat(tTl[:, w, :, :]), bank[:, 4, :], f32(flat(tTh[:, w, :, :])), ALU.subtract).then_inc(turn_lo, 1)

            def qk(s, a):
                for n, (hi, lo, b) in enumerate(((qh, ql, 5), (kh, kl, 6))):
                    wait(qk_hi, "qk", 4, 2 - 2 * n)
                    for m in range(DC):
                        bc = bcol("q%d" % a, m) if n == 0 else (bcol("k0", m) if a == 0 else col("bk1", m))
                        stt(lo[:, s, m, :], halved(b)[:, m, :], bc, f32(hi[:, s, m, :]), ALU.add, ALU.subtract).then_inc(qk_lo, 1)

            def score(s, a, h):
                if h >= SLOTS:
                    wait(turn_p_mm, "turn_p", 1, 1)
                if h == 0:
                    wait(mask_bias, "prep", 4)
                wait(score_mm, "score", alone=True)
                for r in range(RT):
                    e.tensor_tensor_reduce(S[:, h % SLOTS, r, :], halved(h % 2)[:, r, :], nbias[s][a][:, r, :], 1.0, 3.3e38,
                                           ALU.add, ALU.min, nmax[:, h % SLOTS, r:r + 1]).then_inc(score_max, 1)

            def heads(s, a):
                wait(pv_mm, "pv")
                e.reciprocal(flat(rec[:, :, :]), flat(rsum[:, :, :])).then_inc(rec_ok, 1)
                wait(rec_ok, "heads")
                tt(flat(nx[:, s, :, :]).rearrange("p (n e) -> p n e", e=HD),
                   bank[:, 3, :].rearrange("p (n e) -> p n e", e=HD),
                   flat(rec[:, :, :]).unsqueeze(2).to_broadcast([P, RT * H, HD]), ALU.mult).then_inc(heads_ok, 1)

            def proj(s, name):
                if name == "o0" and t.i is not None:
                    wait(stored[s], ("store", s), 16)
                wait(proj_mm, "proj")
                wait(res_ok, "residual")
                tt(flat(y[:, s, :, :]), bank[:, 5, :], flat(res[:, s, :, :]), ALU.add).then_inc(proj_ok, 1)

            def low(slot, done):
                tt(hl[:, slot, :], hf[:, slot, :], f32(hh[:, slot, :]), ALU.subtract).then_inc(done, 1)

            def up(s, j):
                wait(up_hi, "up")
                low(j % 2, up_lo)

            def agg_low(s, d):
                wait(agg_hi, "agg", 1, 1 if d == 0 else 0)
                low(d % 2, agg_lo)

            def mlp_sum(s):
                wait(down_mm, "down")
                wait(res_ok, "residual")
                tt(flat(y[:, s, :, :]), bank[:, 5, :], flat(res[:, s, :, :]), ALU.add).then_inc(sum_ok, 1)

            def a2(s):
                wait(a2_hi, "a2")
                tt(flat(kl[:, s, :, :]), bank[:, 5, :], f32(flat(kh[:, s, :, :])), ALU.subtract).then_inc(a2_lo, 1)

            def score2(s):
                wait(score2_mm, "score2", alone=True)
                for r in range(RT):
                    e.tensor_tensor_reduce(hf[:, 0, r * D:r * D + D], halved(6)[:, r, :], nbias[s][1][:, r, :],
                                           keep[:, s, r:r + 1], 3.3e38, ALU.add, ALU.min, nmax2[:, r:r + 1]).then_inc(score2_max, 1)

            def z2(s):
                wait(z2_mm, "z2")
                e.reciprocal(rec2[:, :], rsum2[:, :]).then_inc(rec2_ok, 1)
                wait(rec2_ok, "z2")
                for r in range(RT):
                    tsc(y[:, s, r, :], halved(5)[:, r, :], rec2[:, r:r + 1], None, ALU.mult).then_inc(z2_ok, 1)

            def hidden(s):
                wait(hid_hi, "hidden")
                tt(flat(hidl[s]), flat(nx[:, s, :, :]), f32(flat(hidh[s])), ALU.subtract).then_inc(hid_lo, 1)

            def masks(s):
                wait(adjT_ok, "turn_adj")
                for l in range(LABELS):
                    tsc(flat(mask[s][l]), flat(adjT[s]), float(l + 1), None, ALU.is_equal).then_inc(mask_ok, 1)

            def count(s):
                wait(cnt_mm, "count")
                tsc(rcnt[:, :], bank[:, 6, 0:LABELS * RT * CW:CW], AGG_EPS, None, ALU.add).then_inc(cnt_eps, 1)
                wait(cnt_eps, "count")
                e.reciprocal(rcnt[:, :], rcnt[:, :]).then_inc(rc_ok, 1)
                wait(rc_ok, "count")
                for n in range(LABELS * RT):
                    ins = tsc(rspread[s][n // (2 * RT)][:, n % (2 * RT), :], ones[:, :], rcnt[:, n:n + 1], None, ALU.mult)
                ins.then_inc(rcol_ok, 1)

            def agg(s, d):
                wait(agg_mm, "agg")
                wait(spread_ok, "spread")
                if d >= 2:
                    wait(agg_lo, "agg_low", 1, 1)
                tt(hf[:, d % 2, :].rearrange("p (c m) -> p c m", c=DC), halved(6 + d % 2),
                   rc[:, d, :].unsqueeze(1).to_broadcast([P, DC, D]), ALU.mult).then_inc(agg_ok, 1)

            def relu(s):
                wait(relu_hi, "relu")
                low(0, relu_lo)

            def gates(s):
                r, n = hf[:, 1, :], flat(res[:, s, :, :])
                wait(gate_act, "gates", 6, 2)
                stt(r, r, 1.0, n, ALU.add, ALU.mult).then_inc(pre_ok, 1)
                wait(pre_ok, "gates", 2, 1)
                wait(out_mm, "gates_out", 3)
                tt(r, bank[:, 4, :], r, ALU.add).then_inc(pre_ok, 1)

            walk(e, t, {"keeps": keeps, "stats": stats, "centre": centre, "norm": norm, "turn": turn, "qk": qk,
                        "score": score, "heads": heads, "proj": proj, "mlp_sum": mlp_sum, "a2": a2, "score2": score2,
                        "z2": z2, "hidden": hidden, "masks": masks, "count": count, "agg": agg, "relu": relu,
                        "up": up, "agg_low": agg_low, "gates": gates})

        @block.tensor
        def _(e):
            t = Tally(loops)
            wait = waiter(e, t)

            def mm3(dst, left, right, first=True, last=True, shared=False):
                (lh, ll), (rh, rl) = left, right
                e.matmul(dst, lh, rh, start=first, stop=False, skip_group_check=shared)
                e.matmul(dst, lh, rl, start=False, stop=False, skip_group_check=shared)
                return e.matmul(dst, ll, rh, start=False, stop=last, skip_group_check=shared)

            def w2(name, c, lo, n):
                return wt(WH, name, c, lo, lo + n), wt(WL, name, c, lo, lo + n)

            def tT(c, lo=0, n=D, new=0):
                return tTh[:, new, c, lo:lo + n], tTl[:, new, c, lo:lo + n]

            def by_feature(b, name, m, first=True, last=True, shared=False, new=0):
                for c in range(DC):
                    ins = mm3(halved(b)[:, m, :], w2(name, c, m * P, P), tT(c, new=new), first and c == 0,
                              last and c == DC - 1, shared)
                return ins

            def by_row(b, name, new=0):
                for r in range(RT):
                    for c in range(DC):
                        ins = mm3(halved(b)[:, r, :], tT(c, r * P, P, new), w2(name, c, 0, D), c == 0, c == DC - 1)
                return ins

            def staged(j, block, c, lo, n, width=D):
                a = block * D + c * width + lo
                return stages[j % 2][:, a:a + n]

            e.wait_ge(s_vecs, 32)
            e.wait_ge(s_staged[0], 16)
            for n in range(3):
                for m in range(DC):
                    for c in range(DC):
                        ins = e.matmul(bank[:, 4, DC * n + m:DC * n + m + 1], staged(0, DC * n, c, m * P, P), col("ln1_b", c),
                                       start=c == 0, stop=c == DC - 1)
            ins.then_inc(s_fold, 1)
            e.wait_ge(s_vb, DC)
            for c in range(DC):
                ins = e.matmul(bank[:, 5, 0:D], vb[:, c, :], staged(0, 3 * DC, c, 0, D), start=c == 0, stop=c == DC - 1)
            ins.then_inc(s_fold, 1)
            e.wait_ge(s_staged[1], 16)
            for f in range(FF // P):
                for c in range(DC):
                    ins = e.matmul(bank[:, 6, f:f + 1], staged(1, 0, c, f * P, P, FF), col("ln2_b", c),
                                   start=c == 0, stop=c == DC - 1)
            ins.then_inc(s_fold, 1)
            e.wait_ge(s_staged[1], 32)
            e.wait_ge(s_vb, 2 * DC)
            for c in range(DC):
                ins = e.matmul(bank[:, 7, 0:D], vb[:, c, :], staged(3, 3 * DC, c, 0, D), start=c == 0, stop=c == DC - 1)
            ins.then_inc(s_fold, 1)
            e.wait_ge(s_staged[1], 64)
            e.wait_ge(s_scaled, len(SCALED))
            for n in range(2):
                for m in range(DC):
                    for c in range(DC):
                        ins = e.matmul(halved(4 + n)[:, m, :], staged(7, 2 * DC * n, c, m * P, P), staged(7, 2 * DC * n + DC, c, 0, D),
                                       start=c == 0, stop=c == DC - 1)
                ins.then_inc(s_prod, 1)
            e.wait_ge(s_wlo, len(GROUPS) + 1)
            e.wait_ge(s_ident, 1)

            def turn(s, src):
                rows = y if src in ("sum", "z2") else nx
                if src == "heads":
                    wait(heads_ok, "heads")
                    if t.recent("gates"):
                        wait(pre_ok, "gates", 2)
                        wait(mix_ok, "gates", 5, 4)
                elif src in ("norm", "in"):
                    wait(norm_ok, "norm", 2)
                elif src == "sum":
                    wait(sum_ok, "mlp_sum")
                else:
                    wait(z2_ok, "z2", 2)
                if src == "in" and t.i is not None:
                    wait(relu_ok, "relu", 2)
                for c in range(DC):
                    for r in range(RT):
                        ins = e.transpose(halved(4)[:, c, r * P:r * P + P], rows[:, s, r, c * P:c * P + P], ident[:, :])
                ins.then_inc(turn_mm, 1)

            def qk(s, a):
                wait(turn_lo, "turn")
                if a == 0 and t.i is not None:
                    wait(gate_act, "gates", 6)
                for b, name in ((5, "q%d" % a), (6, "k%d" % a)):
                    for m in range(DC):
                        ins = by_feature(b, name, m, new=int(a == 0))
                    ins.then_inc(qk_mm, 1)

            def v(s, a):
                by_row(7, "v%d" % a, int(a == 0)).then_inc(v_mm, 1)

            def score(s, a, h):
                c, p = h // HPC, h % HPC * HD
                if h == 0:
                    wait(qk_lo, "qk", 4)
                if h >= 2:
                    wait(score_max, "score", 2, 4)
                for r in range(RT):
                    ins = mm3(halved(h % 2)[:, r, :],
                              (qh[p:p + HD, s, c, r * P:r * P + P], ql[p:p + HD, s, c, r * P:r * P + P]),
                              (kh[p:p + HD, s, c, :], kl[p:p + HD, s, c, :]))
                ins.then_inc(score_mm, 1)

            def turn_p(s, a, h):
                wait(prob_ok, "score", 2, 2 * (min(h + 1, H - 1) - h))
                if h >= 1:
                    wait(turn_p_ok, "turn_p", 1, 1)
                for k in range(DC):
                    for r in range(RT):
                        ins = e.transpose(halved(2)[:, k, r * P:r * P + P], S[:, h % SLOTS, r, k * P:k * P + P], ident[:, :])
                ins.then_inc(turn_p_mm, 1)

            def pv(s, a, h):
                if h == 0:
                    wait(v_ok, "v")
                wait(turn_p_ok, "turn_p", 1, 1 if h + 1 < H else 0)
                for r in range(RT):
                    for k in range(DC):
                        ins = e.matmul(halved(3)[:, r, h * HD:h * HD + HD], PT[:, h % 2, k, r * P:r * P + P],
                                       V[:, s, k, h * HD:h * HD + HD], start=k == 0, stop=k == DC - 1)
                ins.then_inc(pv_mm, 1)

            def proj(s, name):
                wait(turn_lo, "turn")
                by_row(5, name).then_inc(proj_mm, 1)

            def up(s, j):
                wait(turn_lo, "turn")
                if j == 0 and t.recent("gates"):
                    wait(cent_ok, "centre", 2)
                if j >= 2:
                    wait(up_act, "up", 2, 4)
                for f in range(2):
                    for c in range(DC):
                        ins = mm3(halved(6 + j % 2)[:, f, :], w2("w1", c, (2 * j + f) * P, P), tT(c), c == 0, c == DC - 1)
                ins.then_inc(up_mm, 1)

            def down(s, j):
                wait(up_lo, "up", 1, min(j + 2, UPS - 1) - j)
                for f in range(2):
                    for r in range(RT):
                        at = f * D + r * P
                        ins = mm3(halved(5)[:, r, :], (hh[:, j % 2, at:at + P], hl[:, j % 2, at:at + P]),
                                  w2("w2", 2 * j + f, 0, D), (j, f, r) == (0, 0, 0), (j, f) == (UPS - 1, 1), True)
                ins.then_inc(down_mm, 1)

            def a2(s):
                wait(turn_lo, "turn")
                for m in range(DC):
                    ins = by_feature(5, "qk2", m)
                ins.then_inc(a2_mm, 1)

            def score2(s):
                wait(a2_lo, "a2")
                if t.recent("gates"):
                    wait(cent_ok, "centre", 2)
                for r in range(RT):
                    for c in range(DC):
                        ins = mm3(halved(6)[:, r, :], (kh[:, s, c, r * P:r * P + P], kl[:, s, c, r * P:r * P + P]), tT(c),
                                  c == 0, c == DC - 1)
                ins.then_inc(score2_mm, 1)

            def turn_p2(s):
                wait(prob2_ok, "score2", 2)
                for k in range(DC):
                    for r in range(RT):
                        ins = e.transpose(halved(7)[:, k, r * P:r * P + P], hf[:, 0, r * D + k * P:r * D + k * P + P], ident[:, :])
                ins.then_inc(turn_p2_mm, 1)

            def z2(s):
                wait(turn_p2_ok, "turn_p2")
                for r in range(RT):
                    for k in range(DC):
                        ins = e.matmul(halved(5)[:, r, :], hf[:, 1, k * D + r * P:k * D + r * P + P], nx[:, s, k, :],
                                       start=k == 0, stop=k == DC - 1)
                ins.then_inc(z2_mm, 1)

            def turn_adj(s):
                wait(v_ok, "v")
                if t.recent("gates"):
                    wait(gate_act, "gates", 6)
                for k in range(DC):
                    for r in range(RT):
                        ins = e.transpose(halved(7)[:, k, r * P:r * P + P], adjf[s][:, r, k * P:k * P + P], ident[:, :])
                ins.then_inc(adjT_mm, 1)

            def count(s):
                wait(mask_ok, "masks", LABELS)
                for l in range(LABELS):
                    for r in range(RT):
                        at = (l * RT + r) * CW
                        for k in range(DC):
                            ins = e.matmul(bank[:, 6, at:at + CW], mask[s][l][:, k, r * P:r * P + P], ones_r[:, :],
                                           start=k == 0, stop=k == DC - 1)
                ins.then_inc(cnt_mm, 1)

            def spread(s, p):
                wait(rcol_ok, "count")
                for n in range(2 * RT):
                    ins = e.transpose(bank[:, 6 + p, n * P:n * P + P], rspread[s][p][:, n, :], ident[:, :])
                ins.then_inc(spread_mm, 1)

            def agg(s, d):
                if d == 0:
                    wait(spread_ok, "spread")
                wait(hid_lo, "hidden")
                if d >= 2:
                    wait(agg_ok, "agg", 1, 2)
                for c in range(DC):
                    for k in range(DC):
                        for n, half in enumerate((hidh[s], hidl[s])):
                            ins = e.matmul(halved(6 + d % 2)[:, c, :], half[:, k, c * P:c * P + P], mask[s][d][:, k, :],
                                           start=(k, n) == (0, 0), stop=(k, n) == (DC - 1, 1))
                ins.then_inc(agg_mm, 1)

            def wd(s, d):
                if d == 0:
                    wait(turn_lo, "turn")
                wait(agg_lo, "agg_low", 1, 1 if d == 0 else 0)
                for c in range(DC):
                    for m in range(DC):
                        ins = mm3(halved(4)[:, m, :], w2("wd", DC * d + c, m * P, P),
                                  (hh[:, d % 2, c * D:c * D + D], hl[:, d % 2, c * D:c * D + D]),
                                  (d, c, m) == (0, 0, 0), (d, c) == (LABELS - 1, DC - 1), True)
                ins.then_inc(wd_mm, 1)

            def gates_hid(s, which):
                if which == "r":
                    wait(turn_lo, "turn")
                    for m in range(DC):
                        by_feature(5, "rh", m, first=m == 0, last=False, shared=True)
                else:
                    for m in range(DC):
                        by_feature(6, "zh", m, first=m == 0, last=False, shared=True)
                    for m in range(DC):
                        ins = by_feature(7, "nh", m)
                    ins.then_inc(hid_mm, 1)

            def gates_out(s):
                wait(relu_lo, "relu")
                for b, name, fresh in ((5, "ri", False), (6, "zi", False), (4, "ni", True)):
                    if fresh and t.i is not None:
                        wait(turn_lo, "turn")
                    for m in range(DC):
                        for c in range(DC):
                            ins = mm3(halved(b)[:, m, :], w2(name, c, m * P, P),
                                      (hh[:, 0, c * D:c * D + D], hl[:, 0, c * D:c * D + D]),
                                      fresh and c == 0, c == DC - 1, not fresh)
                    ins.then_inc(out_mm, 1)

            def turn_back(s):
                wait(mix_ok, "gates", 5)
                wait(qk_lo, "qk", 4)
                for r in range(RT):
                    for c in range(DC):
                        ins = e.transpose(halved(6)[:, r, c * P:c * P + P], y[:, s, c, r * P:r * P + P], ident[:, :])
                ins.then_inc(back_mm, 1)

            walk(e, t, {"turn": turn, "qk": qk, "v": v, "score": score, "turn_p": turn_p, "pv": pv, "proj": proj,
                        "up": up, "down": down, "a2": a2, "score2": score2, "turn_p2": turn_p2, "z2": z2,
                        "turn_adj": turn_adj, "count": count, "spread": spread, "agg": agg, "wd": wd, "gates_hid": gates_hid,
                        "gates_out": gates_out, "turn_back": turn_back})


def kernel(**inputs):
    import numpy as _np
    import concourse.bacc as _bacc
    from concourse import mybir as _mybir
    from concourse.bass_utils import run_bass_kernel_spmd as _run

    a = {k: _np.asarray(v) for k, v in inputs.items()}

    def chunks(w):
        return w.reshape(w.shape[0] // P, P, w.shape[1]).transpose(1, 0, 2).reshape(P, -1)

    mats = {"q0": a["L0_gnn_wq"], "k0": a["L0_gnn_wk"], "v0": a["L0_gnn_wv"], "o0": a["L0_gnn_wo"],
            "w1": a["L0_gnn_w1"], "w2": a["L0_gnn_w2"],
            "q1": a["L1_gnn_Wq"], "k1": a["L1_gnn_Wk"], "v1": a["L1_gnn_Wv"], "o1": a["L1_gnn_Wo"],
            "wd": a["L3_gnn_Wd"].T, "ri": a["L3_gnn_Wri"].T, "rh": a["L3_gnn_Wrh"].T, "zi": a["L3_gnn_Wzi"].T,
            "zh": a["L3_gnn_Wzh"].T, "ni": a["L3_gnn_Wni"].T, "nh": a["L3_gnn_Wnh"].T,
            "q2T": a["L2_gnn_Wq"].T, "k2T": a["L2_gnn_Wk"].T, "v2T": a["L2_gnn_Wv"].T, "o2": a["L2_gnn_Wo"]}
    vecs = {"ln1_g": a["L0_gnn_ln1_g"], "ln1_b": a["L0_gnn_ln1_b"], "ln2_g": a["L0_gnn_ln2_g"], "ln2_b": a["L0_gnn_ln2_b"],
            "bq0": a["L0_gnn_bq"], "bk0": a["L0_gnn_bk"], "bv0": a["L0_gnn_bv"],
            "bq1": a["L1_gnn_bq"], "bk1": a["L1_gnn_bk"], "bv1": a["L1_gnn_bv"],
            "bd": a["L3_gnn_bd"], "bri": a["L3_gnn_bri"], "brh": a["L3_gnn_brh"], "bzi": a["L3_gnn_bzi"],
            "bzh": a["L3_gnn_bzh"], "bni": a["L3_gnn_bni"], "bnh": a["L3_gnn_bnh"], "b1": a["L0_gnn_b1"]}
    rowv = {"bo0": a["L0_gnn_bo"], "b2": a["L0_gnn_b2"], "bo1": a["L1_gnn_bo"], "bo2": a["L2_gnn_bo"],
            "g1": a["L1_gnn_gamma"], "be1": a["L1_gnn_beta"], "g2": a["L2_gnn_gamma"], "be2": a["L2_gnn_beta"],
            "g3": a["L3_gnn_gamma"], "be3": a["L3_gnn_beta"]}
    arrays = {
        "x": _np.ascontiguousarray(a["x"]),
        "adj": _np.ascontiguousarray(a["adj"]),
        "weights": _np.concatenate([chunks(mats[n]) for g in GROUPS for n in g], axis=1),
        "cols": _np.ascontiguousarray(_np.concatenate([vecs[n].reshape(-1, P) for n in COLS]).T),
        "rows": _np.ascontiguousarray(_np.broadcast_to(_np.stack([rowv[n] for n in ROWV]), (P, len(ROWV), D))),
    }
    nc = _bacc.Bacc("TRN2", target_bir_lowering=False, num_devices=1)
    args = [nc.dram_tensor(n, v.shape, _mybir.dt.from_np(v.dtype), kind="ExternalInput").ap() for n, v in arrays.items()]
    args.append(nc.dram_tensor("out", a["x"].shape, _mybir.dt.float32, kind="ExternalOutput").ap())
    build(nc, *args)
    r = _run(nc, [arrays], core_ids=[0])
    return r.results[0]["out"]
```
